# Optimizing a Trainium2 kernel written in Bass

```python
import numpy as np
import jax
import jax.numpy as jnp

def _softmax(x, axis=-1):
    return jax.nn.softmax(x, axis=axis)

def _gelu(x):
    return jax.nn.gelu(x, approximate=True)

def _silu(x):
    return jax.nn.silu(x)

def _sigmoid(x):
    return jax.nn.sigmoid(x)

def _layernorm(x, axis=-1, eps=1e-05):
    m = jnp.mean(x, axis=axis, keepdims=True)
    v = jnp.var(x, axis=axis, keepdims=True)
    return (x - m) / jnp.sqrt(v + eps)

def _scatter_add(tgt, idx, src, axis=0):
    return tgt.at[idx].add(src)

def _segment_sum(src, seg, n):
    return jax.ops.segment_sum(src, seg, n)
kernel_name = 'mk_adaln_ffn_d1_seqx_r8_8c658a'

def setup_inputs(seed: int=0):
    np.random.seed(seed)
    _w = jnp.asarray

    def _rec_inputs():
        import jax
        import jax.numpy as jnp
        _rk = jax.random.key(seed)
        x = 7.22e-05 + 1 * jax.random.normal(jax.random.fold_in(_rk, 1), (8, 128, 512), jnp.float32)
        _lenS = 128 - jax.random.randint(jax.random.fold_in(_rk, 7), (8,), 0, max(1, 128 // 4) + 1, jnp.int32)
        _lenS2 = 128 - jax.random.randint(jax.random.fold_in(_rk, 8), (8,), 0, max(1, 128 // 4) + 1, jnp.int32)
        condB_coeff = 0.00219231 + 0.0100837 * jax.random.normal(jax.random.fold_in(_rk, 11), (8,), jnp.float32)
        _validS = jnp.arange(128)[None, :] < _lenS[:, None]
        _validS2 = jnp.arange(128)[None, :] < _lenS2[:, None]
        _causal = jnp.tril(jnp.ones((128, 128), dtype=bool))
        mask_Bx4096x4096_ik1 = jnp.where(jnp.ones((8, 512, 512), dtype=bool), 1, 0).astype(jnp.int32)
        return (x, condB_coeff, mask_Bx4096x4096_ik1)
    x, condB_coeff, mask_Bx4096x4096_ik1 = _rec_inputs()

    def _L0_cond_setup():
        import jax, jax.numpy as jnp
        import numpy as np
        B, S, D_IN, D_OUT = (4, 64, 512, 512)
        key = jax.random.key(seed)
        k1, k2, k3, k4, k5 = jax.random.split(key, 5)
        hidden_states = jax.random.normal(k1, (B, S, D_IN), dtype=jnp.float32)
        W = jax.random.normal(k2, (D_OUT, D_IN), dtype=jnp.float32) * 0.02
        b = jax.random.normal(k3, (D_OUT,), dtype=jnp.float32) * 0.02
        coeff = jax.random.normal(k4, (B,), dtype=jnp.float32) * 0.01
        mask = jax.random.randint(k5, (B, D_IN, D_OUT), 0, 2, dtype=jnp.int32)
        return {'hidden_states': hidden_states, 'W': W, 'b': b, 'coeff': coeff, 'mask': mask}
    _L0_cond_all = _L0_cond_setup()
    _L0_cond_in = {k: v for k, v in _L0_cond_all.items() if k in ('W', 'b')}
    del _L0_cond_all

    def _L0_ffn_setup():
        import jax, jax.numpy as jnp
        import numpy as np
        H = 512
        I = 256
        E = 16
        TOPK = 4
        SI = 256
        key = jax.random.key(seed)
        ks = jax.random.split(key, 9)
        s = 0.02
        return {'hidden_states': jax.random.normal(ks[0], (2, 256, H), dtype=jnp.float32), 'gate_w': jax.random.normal(ks[1], (E, H), dtype=jnp.float32) * s, 'bias': jnp.zeros((E,), dtype=jnp.float32), 'Wg': jax.random.normal(ks[2], (E, I, H), dtype=jnp.float32) * s, 'Wu': jax.random.normal(ks[3], (E, I, H), dtype=jnp.float32) * s, 'Wd': jax.random.normal(ks[4], (E, H, I), dtype=jnp.float32) * s, 'Sg': jax.random.normal(ks[5], (SI, H), dtype=jnp.float32) * s, 'Su': jax.random.normal(ks[6], (SI, H), dtype=jnp.float32) * s, 'Sd': jax.random.normal(ks[7], (H, SI), dtype=jnp.float32) * s}
    _L0_ffn_all = _L0_ffn_setup()
    _L0_ffn_in = {k: v for k, v in _L0_ffn_all.items() if k in ('gate_w', 'bias', 'Wg', 'Wu', 'Wd', 'Sg', 'Su', 'Sd')}
    del _L0_ffn_all
    return {'x': x, 'condB_coeff': condB_coeff, 'mask_Bx4096x4096_ik1': mask_Bx4096x4096_ik1, 'L0_cond_W': _L0_cond_in['W'], 'L0_cond_b': _L0_cond_in['b'], 'L0_ffn_gate_w': _L0_ffn_in['gate_w'], 'L0_ffn_bias': _L0_ffn_in['bias'], 'L0_ffn_Wg': _L0_ffn_in['Wg'], 'L0_ffn_Wu': _L0_ffn_in['Wu'], 'L0_ffn_Wd': _L0_ffn_in['Wd'], 'L0_ffn_Sg': _L0_ffn_in['Sg'], 'L0_ffn_Su': _L0_ffn_in['Su'], 'L0_ffn_Sd': _L0_ffn_in['Sd']}

def reference(x, condB_coeff, mask_Bx4096x4096_ik1, L0_cond_W, L0_cond_b, L0_ffn_gate_w, L0_ffn_bias, L0_ffn_Wg, L0_ffn_Wu, L0_ffn_Wd, L0_ffn_Sg, L0_ffn_Su, L0_ffn_Sd):
    import jax
    import jax.numpy as jnp

    def _L0_cond_ref(hidden_states, W, b, coeff, mask):
        import jax, jax.numpy as jnp
        import numpy as np
        B, S, D_IN, D_OUT = (4, 64, 512, 512)
        output = jnp.einsum('bsi,oi->bso', hidden_states, W) + b
        sign = (2 * mask - 1).astype(hidden_states.dtype)
        diff = jnp.einsum('bsi,bio->bso', hidden_states, sign)
        return output + diff * coeff[:, None, None]

    def _L0_ffn_ref(hidden_states, gate_w, bias, Wg, Wu, Wd, Sg, Su, Sd):
        import jax, jax.numpy as jnp
        import numpy as np
        H = 512
        I = 256
        E = 16
        TOPK = 4
        SI = 256
        orig_shape = hidden_states.shape
        x = hidden_states.reshape(-1, orig_shape[-1])
        scores = jax.nn.sigmoid(x @ gate_w.T) + bias
        topk_w, topk_idx = jax.lax.top_k(scores, TOPK)
        topk_w = topk_w / (jnp.sum(topk_w, axis=-1, keepdims=True) + 1e-20)
        cw = jnp.sum(jax.nn.one_hot(topk_idx, E, dtype=x.dtype) * topk_w[..., None], axis=1)
        g = jnp.einsum('th,eih->eti', x, Wg)
        u = jnp.einsum('th,eih->eti', x, Wu)
        z = jax.nn.silu(g) * u
        zw = z * cw.T[:, :, None]
        out = jnp.einsum('eti,ehi->th', zw, Wd)
        out = out + jax.nn.silu(x @ Sg.T) * (x @ Su.T) @ Sd.T
        return out.reshape(orig_shape)
    x = x + _L0_ffn_ref(_L0_cond_ref(x, L0_cond_W, L0_cond_b, condB_coeff, mask_Bx4096x4096_ik1), L0_ffn_gate_w, L0_ffn_bias, L0_ffn_Wg, L0_ffn_Wu, L0_ffn_Wd, L0_ffn_Sg, L0_ffn_Su, L0_ffn_Sd)
    return x

_drawn_inputs = setup_inputs


def setup_inputs(seed=0):
    import zlib

    import numpy as np

    out = dict(_drawn_inputs(seed))
    spreads = {'L0_ffn_bias': (0.0, 0.8)}
    factors = {'condB_coeff': 6.352,
     'L0_cond_W': 4.691,
     'L0_cond_b': 8.0,
     'L0_ffn_gate_w': 8.0,
     'L0_ffn_Wg': 8.0,
     'L0_ffn_Wu': 8.0,
     'L0_ffn_Wd': 8.0,
     'L0_ffn_Sg': 4.187,
     'L0_ffn_Su': 4.095,
     'L0_ffn_Sd': 4.143}
    for name, (base, spread) in spreads.items():
        noise = np.random.default_rng([zlib.crc32(name.encode()), seed]).standard_normal(out[name].shape)
        drawn = base * np.exp(spread * noise) if base else spread * noise
        out[name] = jnp.asarray(drawn.astype(out[name].dtype))
    for name, factor in factors.items():
        out[name] = (out[name] * factor).astype(out[name].dtype)
    return out
```

```python
from contextlib import ExitStack

import concourse.bass as bass
from concourse import mybir

F32 = mybir.dt.float32
F32R = mybir.dt.float32r
BF16 = mybir.dt.bfloat16
I32 = mybir.dt.int32
U32 = mybir.dt.uint32
ALU = mybir.AluOpType
ACT = mybir.ActivationFunctionType
AX_X = mybir.AxisListType.X

P = 128
LOG_P = 7
TOPK = 4
WORD_BITS = 24
AHEAD = 3
MARK = 64


def const_layout(E, n_slots):
    return {
        "ident": P, "before": P, "ones": P, "column": P, "slot": n_slots, "power": n_slots,
        "expert": E, "upto": E * E, "below": E * E, "run": E + 2, "token1": 1, "trash": 1,
    }


def adaln_ffn(nc, xT, x, coeff, mask, WT, bias_cond, gateT, bias_gate, WguT, WdT, SguT, SdT, consts, out):
    n_tiles = xT.shape[0]
    H = x.shape[2]
    KH = H // P
    E = gateT.shape[2]
    KI = WdT.shape[2]
    I = KI * P
    NT = n_tiles * P
    ROW = H + E
    MIN_SLOTS = TOPK * n_tiles
    MAX_SLOTS = MIN_SLOTS + E - 1
    NS = 2 * WORD_BITS
    assert MAX_SLOTS <= NS
    SH = n_tiles

    with ExitStack() as ctx:
        def sb(name, shape, dt=F32):
            return ctx.enter_context(nc.sbuf_tensor(name, shape, dt))

        def bank(name):
            return ctx.enter_context(nc.psum_tensor(name, [P, 512], F32))

        def sem(name):
            return ctx.enter_context(nc.semaphore(name))

        h_rows = nc.dram_tensor("h_rows", [NT, ROW], F32, kind="Internal").ap()
        sums = nc.dram_tensor("sums", [NT + P, H], F32, kind="Internal").ap()

        raw_gu = [sb(f"raw_gu{i}", [P, KH, 2 * I]) for i in range(2)]
        raw_d = [sb(f"raw_d{i}", [P, KI, H]) for i in range(2)]
        gu_hi = sb("gu_hi", [P, 2, KH, 2 * I], F32R)
        gu_lo = sb("gu_lo", [P, 2, KH, 2 * I], F32R)
        d_hi = sb("d_hi", [P, 2, KI, H], F32R)
        d_lo = sb("d_lo", [P, 2, KI, H], F32R)
        raw_mask = sb("raw_mask", [P, 2, KH * H], I32)
        sign = [sb(f"sign{i}", [P, KH, H], F32R) for i in range(2)]
        raw_xT = [sb(f"raw_xT{i}", [P, KH, P]) for i in range(2)]
        xT_hi = [sb(f"xT_hi{i}", [P, KH, P], F32R) for i in range(2)]
        xT_lo = [sb(f"xT_lo{i}", [P, KH, P], F32R) for i in range(2)]
        h_nat = [sb(f"h_nat{i}", [P, H]) for i in range(2)]
        hT_hi = sb("hT_hi", [P, n_tiles, KH, P], F32R)
        hT_lo = sb("hT_lo", [P, n_tiles, KH, P], F32R)
        b_cond = sb("b_cond", [P, H])
        c_col = sb("c_col", [P, n_tiles])
        x_nat = [t[:].rearrange("p k n -> p (k n)") for t in raw_xT]
        xg = [sb(f"xg{i}", [P, ROW]) for i in range(AHEAD)]
        silu = [sb(f"silu{i}", [P, I]) for i in range(2)]
        zT_hi = [sb(f"zT_hi{i}", [P, KI, P], F32R) for i in range(2)]
        zT_lo = [sb(f"zT_lo{i}", [P, KI, P], F32R) for i in range(2)]
        y = h_nat
        layout = const_layout(E, NS)
        k_all = sb("k_all", [P, sum(layout.values())])
        const, at = {}, 0
        for name, width in layout.items():
            const[name] = k_all[:, at:at + width]
            at += width
        before_r = sb("before_r", [P, P], F32R)
        ones_r = sb("ones_r", [P, P], F32R)
        column_b = sb("column_b", [P, P], BF16)
        slot_b = sb("slot_b", [P, NS, E], BF16)
        raw_gate = sb("raw_gate", [P, KH, E])
        gate_hi = sb("gate_hi", [P, KH, E], F32R)
        gate_lo = sb("gate_lo", [P, KH, E], F32R)
        b_gate = sb("b_gate", [P, E])
        scores = sb("scores", [P, n_tiles, E])
        top8 = sb("top8", [P, n_tiles, 8])
        idx8 = sb("idx8", [P, n_tiles, 8], U32)
        idxf = sb("idxf", [P, n_tiles, 8])
        wsum = sb("wsum", [P, n_tiles])
        winv = sb("winv", [P, n_tiles])
        wk = sb("wk", [P, n_tiles, TOPK])
        cw = sb("cw", [P, n_tiles, E])
        sel = sb("sel", [P, n_tiles, E], F32R)
        sel_all = sb("sel_all", [P, E], F32R)
        pos_i = sb("pos_i", [P, n_tiles * E], I32)
        sl_i = sb("sl_i", [P, n_tiles * E], I32)
        col_f = sb("col_f", [P, n_tiles, E])
        sl_f = sb("sl_f", [P, n_tiles, E])
        sl_b = sb("sl_b", [P, n_tiles, E], BF16)
        nt_i = sb("nt_i", [P, E], I32)
        nt_f = sb("nt_f", [P, E])
        end_f = sb("end_f", [P, E])
        base_f = sb("base_f", [P, E])
        active = sb("active", [P, E])
        active_e = sb("active_e", [P, E])
        rank = sb("rank", [P, E])
        last_run = sb("last_run", [P, 1])
        run_f = sb("run_f", [P, NS])
        run_i = sb("run_i", [1, NS], I32)
        run_odd = sb("run_odd", [1, NS], I32)
        first = sb("first", [P, NS])
        first_i = sb("first_i", [1, NS], I32)
        flags = sb("flags", [P, 2, NS])
        runs_f = sb("runs_f", [P, E + 2])
        runs_i = sb("runs_i", [1, E + 2], I32)
        words_f = sb("words_f", [P, 8])
        words = sb("words", [1, 8], I32)
        hot_e = sb("hot_e", [P, NS, E], BF16)
        AV = sb("AV", [P, n_tiles, 2, NS, E], BF16)
        found = sb("found", [P, NS])
        pad = sb("pad", [P, NS])
        take_i = sb("take_i", [P, NS], U32)
        give_i = sb("give_i", [P, NS], U32)
        cw_row = sb("cw_row", [P, E])
        cw_col = sb("cw_col", [P, MAX_SLOTS])
        scratch = raw_mask[:].rearrange("p a b -> p (a b)")
        B = [scratch[:, i * NT // 2:(i + 1) * NT // 2].bitcast(BF16).rearrange("p (t c) -> p t c", t=n_tiles)
             for i in range(2)]

        def part(start, *shape):
            n = 1
            for d in shape:
                n *= d
            v = scratch[:, start:start + n].bitcast(F32)
            if len(shape) == 2:
                return v.rearrange("p (a b) -> p a b", a=shape[0])
            return v.rearrange("p (a b c) -> p a b c", a=shape[0], b=shape[1])

        hot = part(0, n_tiles, E, TOPK)
        hotw = part(n_tiles * E * TOPK, n_tiles, E, TOPK)
        ended = part(0, NS, E)
        ended_a = part(NS * E, NS, E)
        begun = part(2 * NS * E, NS, E)
        tri = part(3 * NS * E, E, E)
        at_run = part(3 * NS * E, E + 2, E)

        ps_a = [bank(f"ps_a{i}") for i in range(2)]
        ps_b = [bank(f"ps_b{i}") for i in range(2)]
        ps_t = [bank(f"ps_t{i}") for i in range(2)]
        ps_z = bank("ps_z")
        ps_g = bank("ps_g")

        (s_small, s_wst0, s_wst1, s_whi, s_wlo, s_xhi, s_xlo, s_sign, s_cond, s_h, s_hT, s_hThi, s_hTlo,
         s_gate, s_gwhi, s_gwlo, s_sig, s_cw, s_cwst, s_sel, s_pos, s_words, s_dve, s_B, s_list, s_idx,
         s_up, s_silu, s_zmul, s_zT, s_zhi, s_zlo, s_down, s_ysh, s_yex, s_trash,
         s_guhi, s_gulo, s_dhi, s_dlo, s_xgT, s_xghi, s_xglo, s_cwsel, s_scat, s_done, s_out, s_const) = [
            sem(n) for n in (
                "small wst0 wst1 whi wlo xhi xlo sign cond h hT hThi hTlo gate gwhi gwlo sig cw cwst sel pos "
                "words dve B list idx up silu zmul zT zhi zlo down ysh yex trash guhi gulo dhi dlo xgT xghi xglo "
                "cwsel scat done out const").split()]
        s_xT = [sem(f"xT{i}") for i in range(2)]
        s_hst = [sem(f"hst{i}") for i in range(2)]
        s_mask = [sem(f"mask{i}") for i in range(2)]
        s_xnat = [sem(f"xnat{i}") for i in range(2)]
        s_yst = [sem(f"yst{i}") for i in range(2)]
        s_raw = [sem(f"raw{i}") for i in range(2)]
        s_gath = [sem(f"gath{i}") for i in range(AHEAD)]
        N_SMALL = 5

        lists_after = {m: range(4 * (m - 1), 4 * m) for m in range(1, 5)}

        def slots(eng, body):
            count = [None]

            def step(s):
                def more(then, otherwise):
                    if s + 1 < MIN_SLOTS:
                        then()
                        step(s + 1)
                    elif s + 1 == MAX_SLOTS:
                        otherwise()
                    else:
                        with eng.If(count[0] > s + 1):
                            then()
                            step(s + 1)
                        with eng.Else():
                            otherwise()
                body(s, more)

            eng.wait_ge(s_words, 1)
            count[0] = eng.value_load(words[0:1, 0:1], min_val=MIN_SLOTS, max_val=MAX_SLOTS)
            step(0)

        def flag_words(eng, kind):
            return [eng.value_load(words[0:1, 1 + 2 * kind + i:2 + 2 * kind + i], min_val=0, max_val=(1 << WORD_BITS) - 1)
                    for i in range(2)]

        def flag(pair, s):
            return (pair[s // WORD_BITS] >> (s % WORD_BITS)) & 1

        block = ctx.enter_context(nc.Block())

        @block.sync
        def _(sp):
            def tile_in(t):
                if t >= 2:
                    sp.wait_ge(s_xhi, t - 1)
                    sp.wait_ge(s_xlo, t - 1)
                    sp.wait_ge(s_sign, t - 1)
                sp.dma_start(raw_xT[t % 2][:], xT[t]).then_inc(s_xT[t % 2], 16)
                sp.dma_start(raw_mask[:, t % 2, :], mask[t].rearrange("p k n -> p (k n)")).then_inc(s_mask[t % 2], 16)

            sp.dma_start(raw_xT[0][:], xT[0]).then_inc(s_xT[0], 16)
            sp.dma_start(raw_gu[0][:], WT).then_inc(s_wst0, 16)
            sp.dma_start(raw_mask[:, 0, :], mask[0].rearrange("p k n -> p (k n)")).then_inc(s_mask[0], 16)
            for dst, src in ((b_cond[:], bias_cond), (c_col[:], coeff), (raw_gate[:], gateT), (b_gate[:], bias_gate),
                             (k_all[:], consts)):
                sp.dma_start(dst, src).then_inc(s_small, 16)
            tile_in(1)
            for t in range(n_tiles):
                if t + 2 < n_tiles:
                    tile_in(t + 2)
                if t == 3:
                    sp.dma_start(raw_gu[1][:], SguT).then_inc(s_wst1, 16)
                    sp.dma_start(raw_d[1][:], SdT).then_inc(s_wst1, 16)
                sp.wait_ge(s_h, 2 * (t + 1))
                sp.dma_start(h_rows[t * P:(t + 1) * P, 0:H], h_nat[t % 2][:]).then_inc(s_hst[t % 2], 16)
            sp.wait_ge(s_cw, 1)
            sp.dma_start(h_rows.rearrange("(t p) c -> p t c", p=P)[:, :, H:ROW], cw[:]).then_inc(s_cwst, 16)

            def run_in(e1, i):
                sp.dma_start(raw_gu[i][:], WguT[bass.ds(e1 - 1, 1), :, :, :].rearrange("e p k n -> (e p) k n")).then_inc(s_raw[i], 16)
                sp.dma_start(raw_d[i][:], WdT[bass.ds(e1 - 1, 1), :, :, :].rearrange("e p k n -> (e p) k n")).then_inc(s_raw[i], 16)

            sp.wait_ge(s_words, 1)
            sp.wait_ge(s_whi, 2)
            sp.wait_ge(s_wlo, 2)
            for r in range(2):
                run_in(sp.value_load(runs_i[0:1, r:r + 1], min_val=1, max_val=E), r)

            def slot(s, more):
                with sp.If(sp.value_load(first_i[0:1, s:s + 1], min_val=0, max_val=1) > 0):
                    run = sp.value_load(run_i[0:1, s:s + 1], min_val=0, max_val=E - 1)
                    e1 = sp.value_load(runs_i[0:1, bass.ds(run + 2, 1)], min_val=0, max_val=E)
                    with sp.If(e1 > 0):
                        for q in (s_guhi, s_gulo, s_dhi, s_dlo):
                            sp.wait_ge(q, s + 1)
                        known = sp.value_load(runs_i[0:1, bass.ds(run + 2, 1)], min_val=1, max_val=E)
                        with sp.If((run & 1) > 0):
                            run_in(known, 1)
                        with sp.Else():
                            run_in(known, 0)
                more(lambda: None, lambda: None)

            slots(sp, slot)
            sp.wait_ge(s_done, 1)
            sp.dma_start(out.rearrange("t p h -> (t p) h"), sums[0:NT, :]).then_inc(s_out, 16)
            sp.wait_ge(s_out, 16)

        def gather(pool, s):
            if s >= AHEAD:
                pool.wait_ge(s_xgT, s - AHEAD + 1)
                pool.wait_ge(s_cwsel, s - AHEAD + 1)
            pool.indirect_dma_start(xg[s % AHEAD][:], None, h_rows, bass.IndirectOffsetOnAxis(ap=take_i[:, s:s + 1], axis=0))\
                .then_inc(s_gath[s % AHEAD], 16)

        @block.gpsimd
        def _(pool):
            def split_lo(s):
                pool.wait_ge((s_wst0, s_wst1)[s], 16 * (1 + s))
                pool.wait_ge(s_whi, s + 1)
                last = pool.tensor_tensor(gu_lo[:, s], raw_gu[s][:], gu_hi[:, s], ALU.subtract)
                if s:
                    last = pool.tensor_tensor(d_lo[:, s], raw_d[s][:], d_hi[:, s], ALU.subtract)
                last.then_inc(s_wlo, 1)

            split_lo(0)
            for t in range(n_tiles):
                pool.wait_ge(s_mask[t % 2], 16 * (t // 2 + 1))
                if t >= 2:
                    pool.wait_ge(s_cond, t - 1)
                pool.tensor_scalar(sign[t % 2][:], raw_mask[:, t % 2, :], 2, -1, ALU.mult, ALU.add).then_inc(s_sign, 1)
                if t == 5:
                    split_lo(1)

            pool.wait_ge(s_small, 16 * N_SMALL)
            pool.dma_start(sums[NT:NT + P, :], b_cond[:]).then_inc(s_trash, 16)

            def residual_in(m):
                pool.dma_start(x_nat[m % 2], x[m]).then_inc(s_xnat[m % 2], 16)

            pool.wait_ge(s_xhi, n_tiles)
            pool.wait_ge(s_xlo, n_tiles)
            residual_in(0)
            residual_in(1)
            for m in range(SH):
                pool.wait_ge(s_ysh, m + 1)
                pool.dma_start(sums[m * P:(m + 1) * P, :], y[m % 2][:]).then_inc(s_yst[m % 2], 16)
                if m + 2 < SH:
                    residual_in(m + 2)
                if m == SH - 3:
                    pool.wait_ge(s_idx, 1)
                    for q in s_hst:
                        pool.wait_ge(q, 16 * (n_tiles // 2))
                    pool.wait_ge(s_cwst, 16)
                    for s in range(AHEAD):
                        gather(pool, s)
            pool.wait_ge(s_trash, 16)
            for i in range(2):
                pool.wait_ge(s_yst[i], 16 * (SH // 2))

            def scatter(s):
                pool.wait_ge(s_yex, s + 1)
                if s:
                    pool.wait_ge(s_scat, 16 * s)
                pool.indirect_dma_start(sums, bass.IndirectOffsetOnAxis(ap=give_i[:, s:s + 1], axis=0), y[s % 2][:], None,
                                        compute_op=ALU.add).then_inc(s_scat, 16)

            def slot(s, more):
                def otherwise():
                    scatter(s - 2)
                    scatter(s - 1)
                    scatter(s)
                    if s + 1 < MAX_SLOTS:
                        pool.wait_ge(s_gath[(s + 1) % AHEAD], 16 * ((s + 1) // AHEAD + 1))
                    pool.wait_ge(s_scat, 16 * (s + 1))
                    pool.sem_inc(s_done, 1)

                def then():
                    if AHEAD <= s + 2 < MAX_SLOTS:
                        gather(pool, s + 2)
                    if s >= 2:
                        scatter(s - 2)
                more(then, otherwise)

            slots(pool, slot)

        def raw_run_here(eng, s, i):
            run = eng.value_load(run_i[0:1, s:s + 1], min_val=0, max_val=E - 1)
            eng.wait_ge(s_raw[i], (((run + 1) >> 1) + 1) * 32)

        def split_next(eng, word, s, gu, done, counted, before):
            with eng.If(flag(word, s) > 0):
                eng.wait_ge(*before)
                odd = eng.value_load(run_odd[0:1, s:s + 1], min_val=0, max_val=1)
                with eng.If(odd > 0):
                    raw_run_here(eng, s, 0)
                    gu(0).then_inc(done, 1)
                with eng.Else():
                    raw_run_here(eng, s, 1)
                    gu(1).then_inc(done, 1)
            with eng.Else():
                eng.wait_ge(*counted)
                eng.sem_inc(done, 1)

        @block.scalar
        def _(act):
            def split_hi(s):
                act.wait_ge((s_wst0, s_wst1)[s], 16 * (1 + s))
                last = act.copy(gu_hi[:, s], raw_gu[s][:])
                if s:
                    last = act.copy(d_hi[:, s], raw_d[s][:])
                last.then_inc(s_whi, 1)

            def x_hi(t):
                act.wait_ge(s_xT[t % 2], 16 * (t // 2 + 1))
                if t >= 2:
                    act.wait_ge(s_cond, t - 1)
                act.copy(xT_hi[t % 2][:], raw_xT[t % 2][:]).then_inc(s_xhi, 1)

            x_hi(0)
            split_hi(0)
            act.wait_ge(s_small, 16 * N_SMALL)
            act.copy(gate_hi[:], raw_gate[:]).then_inc(s_gwhi, 1)
            for t in range(n_tiles):
                if t + 1 < n_tiles:
                    x_hi(t + 1)
                act.wait_ge(s_hT, t + 1)
                act.copy(hT_hi[:, t], ps_t[t % 2][:]).then_inc(s_hThi, 1)
                if t == 4:
                    split_hi(1)
            act.wait_ge(s_gate, n_tiles)
            act.activation(scores[:], ps_g[:, 0:n_tiles * E], ACT.Sigmoid).then_inc(s_sig, 1)

            def silu_of(m):
                act.wait_ge(s_up, m + 1)
                if m >= 2:
                    act.wait_ge(s_zT, m - 1)
                act.activation(silu[m % 2][:], ps_a[m % 2][:, 0:I], ACT.Silu).then_inc(s_silu, 1)

            def zT_hi_of(m):
                act.wait_ge(s_zT, m + 1)
                if m >= 2:
                    act.wait_ge(s_down, m - 1)
                act.copy(zT_hi[m % 2][:], ps_z[:, 0:I]).then_inc(s_zhi, 1)

            for m in range(SH):
                silu_of(m)
                if m:
                    zT_hi_of(m - 1)
                if m == 5:
                    act.wait_ge(s_raw[0], 32)
                    act.copy(gu_hi[:, 0], raw_gu[0][:]).then_inc(s_guhi, 1)
                    act.copy(d_hi[:, 0], raw_d[0][:]).then_inc(s_dhi, 1)

            def row_hi(s):
                act.wait_ge(s_xgT, s + 1)
                act.wait_ge(s_up, SH + s - 1)
                act.copy(xT_hi[s % 2][:], ps_t[s % 2][:]).then_inc(s_xghi, 1)

            def weighted(s):
                act.wait_ge(s_down, SH + s + 1)
                act.wait_ge(s_cwsel, s + 1)
                if s < 2:
                    act.wait_ge(s_yst[s % 2], 16 * (SH // 2))
                else:
                    act.wait_ge(s_scat, 16 * (s - 1))
                act.activation(y[s % 2][:], ps_b[s % 2][:], ACT.Copy, scale=cw_col[:, s:s + 1]).then_inc(s_yex, 1)

            row_hi(0)
            act.wait_ge(s_words, 1)
            word = flag_words(act, 0)

            def slot(s, more):
                if s >= 2:
                    weighted(s - 2)
                if s:
                    split_next(act, word, s - 1, lambda i: act.copy(d_hi[:, i], raw_d[i][:]), s_dhi,
                               (s_silu, SH + s), (s_down, SH + s - 1))
                zT_hi_of(SH + s - 1)

                def rest():
                    split_next(act, word, s, lambda i: act.copy(gu_hi[:, i], raw_gu[i][:]), s_guhi,
                               (s_silu, SH + s), (s_up, SH + s))
                    silu_of(SH + s)

                def then():
                    row_hi(s + 1)
                    rest()

                def otherwise():
                    silu_of(SH + s)
                    weighted(s - 1)
                    zT_hi_of(SH + s)
                    weighted(s)
                more(then, otherwise)

            slots(act, slot)

        @block.vector
        def _(dve):
            step = [0]

            def link(ins):
                step[0] += 1
                ins.then_inc(s_dve, 1)

            def linked():
                dve.wait_ge(s_dve, step[0])

            def chain(ins):
                link(ins)
                linked()

            dve.wait_ge(s_xT[0], 16)

            def x_lo(t):
                dve.wait_ge(s_xhi, t + 1)
                if t >= 2:
                    dve.wait_ge(s_cond, t - 1)
                dve.tensor_tensor(xT_lo[t % 2][:], raw_xT[t % 2][:], xT_hi[t % 2][:], ALU.subtract).then_inc(s_xlo, 1)

            x_lo(0)
            dve.wait_ge(s_gwhi, 1)
            dve.tensor_tensor(gate_lo[:], raw_gate[:], gate_hi[:], ALU.subtract).then_inc(s_gwlo, 1)
            link(dve.tensor_copy(before_r[:], const["before"]))
            link(dve.tensor_copy(ones_r[:], const["ones"]))
            link(dve.tensor_copy(column_b[:], const["column"]))
            link(dve.tensor_scalar(slot_b[:], const["slot"].unsqueeze(2).broadcast_to([P, NS, E]), float(MARK), None, ALU.add))
            for t in range(n_tiles):
                if t + 1 < n_tiles:
                    x_lo(t + 1)
                dve.wait_ge(s_cond, t + 1)
                dve.wait_ge(s_small, 16 * N_SMALL)
                if t >= 2:
                    dve.wait_ge(s_hT, t - 1)
                    dve.wait_ge(s_hst[t % 2], 16 * (t // 2))
                dve.scalar_tensor_tensor(h_nat[t % 2][:], ps_b[t % 2][:], c_col[:, t:t + 1], b_cond[:],
                                         ALU.mult, ALU.add).then_inc(s_h, 1)
                dve.wait_ge(s_h, 2 * t + 1)
                dve.tensor_tensor(h_nat[t % 2][:], h_nat[t % 2][:], ps_a[t % 2][:], ALU.add).then_inc(s_h, 1)
                dve.wait_ge(s_hThi, t + 1)
                dve.tensor_tensor(hT_lo[:, t], ps_t[t % 2][:], hT_hi[:, t], ALU.subtract).then_inc(s_hTlo, 1)

            dve.wait_ge(s_sig, 1)
            dve.wait_ge(s_sign, n_tiles)
            chain(dve.tensor_tensor(scores[:], scores[:], b_gate[:].unsqueeze(1).broadcast_to([P, n_tiles, E]), ALU.add))
            for t in range(n_tiles):
                link(dve.max(top8[:, t, :], scores[:, t, :]))
            linked()
            for t in range(n_tiles):
                link(dve.max_index(idx8[:, t, :], top8[:, t, :], scores[:, t, :]))
            link(dve.tensor_reduce(wsum[:], top8[:, :, 0:TOPK], AX_X, ALU.add))
            linked()
            link(dve.tensor_copy(idxf[:], idx8[:]))
            chain(dve.tensor_scalar(winv[:], wsum[:], 1e-20, None, ALU.add))
            for t in range(n_tiles):
                link(dve.tensor_tensor(hot[:, t], idxf[:, t, 0:TOPK].unsqueeze(1).broadcast_to([P, E, TOPK]),
                                       const["expert"].unsqueeze(2).broadcast_to([P, E, TOPK]), ALU.is_equal))
            link(dve.reciprocal(wsum[:], winv[:]))
            linked()
            with nc.allow_low_precision(reason="0 and 1"):
                dve.tensor_reduce(sel[:], hot, AX_X, ALU.add).then_inc(s_sel, 1)
            link(dve.tensor_tensor(wk[:], top8[:, :, 0:TOPK], wsum[:].unsqueeze(2).broadcast_to([P, n_tiles, TOPK]), ALU.mult))
            dve.wait_ge(s_sel, 1)
            with nc.allow_low_precision(reason="counts up to the number of tiles"):
                dve.tensor_reduce(sel_all[:], sel[:].bitcast(F32).rearrange("p t e -> p e t"), AX_X, ALU.add).then_inc(s_sel, 1)
            linked()
            for t in range(n_tiles):
                link(dve.tensor_tensor(hotw[:, t], hot[:, t], wk[:, t].unsqueeze(1).broadcast_to([P, E, TOPK]), ALU.mult))
            linked()
            dve.tensor_reduce(cw[:], hotw, AX_X, ALU.add).then_inc(s_cw, 1)
            dve.wait_ge(s_cw, 1)

            def zmul(m):
                dve.wait_ge(s_silu, m + 1)
                dve.tensor_tensor(silu[m % 2][:], silu[m % 2][:], ps_a[m % 2][:, I:2 * I], ALU.mult).then_inc(s_zmul, 1)

            def zT_lo_of(m):
                dve.wait_ge(s_zhi, m + 1)
                if m >= 2:
                    dve.wait_ge(s_down, m - 1)
                dve.tensor_tensor(zT_lo[m % 2][:], ps_z[:, 0:I], zT_hi[m % 2][:], ALU.subtract).then_inc(s_zlo, 1)

            def shared_out(m):
                dve.wait_ge(s_down, m + 1)
                dve.wait_ge(s_xnat[m % 2], 16 * (m // 2 + 1))
                dve.wait_ge(s_hst[m % 2], 16 * (n_tiles // 2))
                if m >= 2:
                    dve.wait_ge(s_yst[m % 2], 16 * (m // 2))
                dve.tensor_tensor(y[m % 2][:], x_nat[m % 2], ps_b[m % 2][:], ALU.add).then_inc(s_ysh, 1)

            def tables():
                dve.wait_ge(s_pos, 1)
                pos, counts = ps_g[:, 0:n_tiles * E], ps_g[:, n_tiles * E:n_tiles * E + E]
                link(dve.tensor_copy(pos_i[:], pos))
                chain(dve.tensor_scalar(nt_i[:], counts, float(P - 1), None, ALU.add))
                chain(dve.tensor_scalar(nt_i[:], nt_i[:], LOG_P, None, ALU.arith_shift_right))
                chain(dve.tensor_copy(nt_f[:], nt_i[:]))
                by_e = [P, E, E]
                upto = const["upto"].rearrange("p (a b) -> p a b", a=E)
                below = const["below"].rearrange("p (a b) -> p a b", a=E)
                chain(dve.tensor_tensor(tri, nt_f[:].unsqueeze(1).broadcast_to(by_e), upto, ALU.mult))
                link(dve.tensor_scalar(active[:], nt_f[:], 1.0, None, ALU.min))
                chain(dve.tensor_reduce(end_f[:], tri, AX_X, ALU.add))
                link(dve.tensor_tensor(base_f[:], end_f[:], nt_f[:], ALU.subtract))
                chain(dve.tensor_tensor(tri, active[:].unsqueeze(1).broadcast_to(by_e), below, ALU.mult))
                by_s = [P, NS, E]
                slot_of = const["slot"].unsqueeze(2).broadcast_to(by_s)
                link(dve.tensor_tensor(ended, slot_of, end_f[:].unsqueeze(1).broadcast_to(by_s), ALU.is_ge))
                chain(dve.tensor_reduce(rank[:], tri, AX_X, ALU.add))
                link(dve.tensor_tensor(ended_a, ended, active[:].unsqueeze(1).broadcast_to(by_s), ALU.mult))
                link(dve.tensor_tensor(active_e[:], active[:], const["expert"], ALU.mult))
                link(dve.tensor_tensor(begun, slot_of, base_f[:].unsqueeze(1).broadcast_to(by_s), ALU.is_ge))
                linked()
                by_r = [P, E + 2, E]
                link(dve.tensor_tensor(active_e[:], active_e[:], active[:], ALU.add))
                link(dve.tensor_reduce(run_f[:], ended_a, AX_X, ALU.add))
                link(dve.tensor_tensor(at_run, rank[:].unsqueeze(1).broadcast_to(by_r),
                                       const["run"].unsqueeze(2).broadcast_to(by_r), ALU.is_equal))
                link(dve.scalar_tensor_tensor(last_run[:], active[:, E - 1:E], -1.0, rank[:, E - 1:E], ALU.add, ALU.add))
                linked()
                link(dve.tensor_tensor(at_run, at_run, active_e[:].unsqueeze(1).broadcast_to(by_r), ALU.mult))
                link(dve.memset(first[:, 0:1], 1.0))
                link(dve.tensor_tensor(first[:, 1:NS], run_f[:, 1:NS], run_f[:, 0:NS - 1], ALU.not_equal))
                link(dve.tensor_copy(run_i[:], run_f[0:1, :]))
                linked()
                link(dve.tensor_reduce(runs_f[:], at_run, AX_X, ALU.add))
                link(dve.tensor_scalar(run_odd[:], run_i[:], 1, None, ALU.bitwise_and))
                link(dve.tensor_copy(first_i[:], first[0:1, :]))
                link(dve.tensor_scalar(flags[:, 0, :], run_f[:], last_run[:, 0:1], None, ALU.is_lt))
                linked()
                link(dve.tensor_copy(runs_i[:], runs_f[0:1, :]))
                link(dve.tensor_tensor(flags[:, 0, :], flags[:, 0, :], first[:], ALU.mult))
                link(dve.tensor_copy(flags[0:1, 1, :], run_odd[:]))
                linked()
                chain(dve.tensor_tensor(flags[0:1], flags[0:1], const["power"][0:1].unsqueeze(1).broadcast_to([1, 2, NS]), ALU.mult))
                link(dve.tensor_copy(words_f[0:1, 0:1], end_f[0:1, E - 1:E]))
                chain(dve.tensor_reduce(words_f[0:1, 1:5], flags[0:1].rearrange("p k (w b) -> p (k w) b", w=2), AX_X, ALU.add))
                dve.tensor_copy(words[0:1, 0:5], words_f[0:1, 0:5]).then_inc(s_words, 1)

            def places():
                link(dve.tensor_tensor(hot_e[:], begun, ended, ALU.subtract))
                chain(dve.tensor_scalar(sl_i[:], pos_i[:], LOG_P, None, ALU.arith_shift_right))
                link(dve.tensor_copy(sl_f[:], sl_i[:]))
                chain(dve.tensor_scalar(pos_i[:], pos_i[:], P - 1, None, ALU.bitwise_and))
                link(dve.tensor_copy(col_f[:], pos_i[:]))
                chain(dve.tensor_tensor(sl_f[:], sl_f[:], base_f[:].unsqueeze(1).broadcast_to([P, n_tiles, E]), ALU.add))
                chain(dve.scalar_tensor_tensor(sl_b[:], sel[:].bitcast(F32), float(MARK), sl_f[:], ALU.mult, ALU.add))
                for t in range(n_tiles):
                    link(dve.tensor_tensor(AV[:, t, 1], sl_b[:, t].unsqueeze(1).broadcast_to([P, NS, E]), slot_b[:], ALU.is_equal))
                linked()
                for t in range(n_tiles):
                    link(dve.tensor_scalar(AV[:, t, 0], AV[:, t, 1], const["token1"], None, ALU.mult))
                linked()
                for t in range(n_tiles):
                    link(dve.tensor_scalar(AV[:, t, 1], AV[:, t, 1], float(t), None, ALU.mult))
                linked()

            def columns(e):
                if e >= 2:
                    dve.wait_ge(s_list, e - 1)
                for t in range(n_tiles):
                    last = dve.tensor_scalar(B[e % 2][:, t, :], column_b[:], col_f[:, t, e:e + 1], None, ALU.is_equal)
                last.then_inc(s_B, 1)

            def indices():
                dve.wait_ge(s_list, E)
                chain(dve.tensor_copy(pad[:], ps_g[:, 0:NS]))
                chain(dve.scalar_tensor_tensor(found[:], ps_g[:, NS:2 * NS], float(P), pad[:], ALU.mult, ALU.add))
                link(dve.tensor_scalar(pad[:], found[:], 0.0, const["trash"], ALU.is_equal, ALU.mult))
                chain(dve.tensor_scalar(found[:], found[:], -1.0, None, ALU.add))
                link(dve.tensor_scalar(take_i[:], found[:], 0.0, None, ALU.max))
                link(dve.tensor_tensor(give_i[:], found[:], pad[:], ALU.add))
                linked()
                dve.memset(cw_row[:, 0:1], 0.0).then_inc(s_idx, 1)

            for m in range(SH):
                zmul(m)
                if m:
                    zT_lo_of(m - 1)
                    shared_out(m - 1)
                if m == 0:
                    tables()
                if m == 1:
                    places()
                if m in lists_after:
                    for e in lists_after[m]:
                        columns(e)
                if m == 4:
                    indices()
                if m == 5:
                    dve.wait_ge(s_guhi, 1)
                    dve.tensor_tensor(gu_lo[:, 0], raw_gu[0][:], gu_hi[:, 0], ALU.subtract).then_inc(s_gulo, 1)
                    dve.wait_ge(s_dhi, 1)
                    dve.tensor_tensor(d_lo[:, 0], raw_d[0][:], d_hi[:, 0], ALU.subtract).then_inc(s_dlo, 1)

            def row_lo(s):
                dve.wait_ge(s_gath[s % AHEAD], 16 * (s // AHEAD + 1))
                if s:
                    dve.wait_ge(s_cwsel, s)
                dve.tensor_tensor_reduce(cw_row[:], xg[s % AHEAD][:, H:ROW], hot_e[:, s, :], 1.0, 0.0, ALU.mult, ALU.add,
                                         cw_col[:, s:s + 1]).then_inc(s_cwsel, 1)
                dve.wait_ge(s_xghi, s + 1)
                dve.wait_ge(s_up, SH + s - 1)
                dve.tensor_tensor(xT_lo[s % 2][:], ps_t[s % 2][:], xT_hi[s % 2][:], ALU.subtract).then_inc(s_xglo, 1)

            row_lo(0)
            word = flag_words(dve, 0)

            def less(i, lo, raw, hi, done, s):
                dve.wait_ge(done, s)
                return dve.tensor_tensor(lo[:, i], raw[i][:], hi[:, i], ALU.subtract)

            def slot(s, more):
                if s:
                    split_next(dve, word, s - 1, lambda i: less(i, d_lo, raw_d, d_hi, s_dhi, s + 1), s_dlo,
                               (s_zmul, SH + s), (s_down, SH + s - 1))
                zT_lo_of(SH + s - 1)

                def then():
                    row_lo(s + 1)
                    split_next(dve, word, s, lambda i: less(i, gu_lo, raw_gu, gu_hi, s_guhi, s + 2), s_gulo,
                               (s_zmul, SH + s), (s_up, SH + s))
                    zmul(SH + s)
                    if s == 0:
                        shared_out(SH - 1)

                def otherwise():
                    zmul(SH + s)
                    zT_lo_of(SH + s)
                more(then, otherwise)

            slots(dve, slot)

        @block.tensor
        def _(pe):
            def product(dst, pairs, which=None):
                n = len(pairs)
                for i in which or range(n):
                    lhs, rhs = pairs[i]
                    last = pe.matmul(dst, lhs, rhs, start=(i == 0), stop=(i == n - 1))
                return last

            def three(lhi, llo, rhi, rlo, chunks):
                hi = [(lhi[:, k], r(k)) for k in range(chunks) for r in (rhi, rlo)]
                return hi + [(llo[:, k], rhi(k)) for k in range(chunks)]

            def fixed(w, *at):
                return lambda k: w[(slice(None),) + at + (k,)]

            def cond(t):
                pe.wait_ge(s_xhi, t + 1)
                pe.wait_ge(s_xlo, t + 1)
                pe.wait_ge(s_whi, 1)
                pe.wait_ge(s_wlo, 1)
                if t >= 2:
                    pe.wait_ge(s_h, 2 * (t - 1))
                i = t % 2
                product(ps_a[i][:], three(xT_hi[i], xT_lo[i], fixed(gu_hi, 0), fixed(gu_lo, 0), KH))
                pe.wait_ge(s_sign, t + 1)
                product(ps_b[i][:], [(h[i][:, k], sign[i][:, k]) for h in (xT_hi, xT_lo) for k in range(KH)]).then_inc(s_cond, 1)

            def turn(t):
                pe.wait_ge(s_h, 2 * (t + 1))
                pe.wait_ge(s_small, 16 * N_SMALL)
                if t >= 2:
                    pe.wait_ge(s_hTlo, t - 1)
                for k in range(KH):
                    last = pe.transpose(ps_t[t % 2][:, k * P:(k + 1) * P], h_nat[t % 2][:, k * P:(k + 1) * P], const["ident"])
                last.then_inc(s_hT, 1)

            def gate(t):
                pe.wait_ge(s_hThi, t + 1)
                pe.wait_ge(s_hTlo, t + 1)
                pe.wait_ge(s_gwlo, 1)
                product(ps_g[:, t * E:(t + 1) * E], three(hT_hi[:, t], hT_lo[:, t], fixed(gate_hi), fixed(gate_lo), KH))\
                    .then_inc(s_gate, 1)

            for t in range(n_tiles + 2):
                if t < n_tiles:
                    cond(t)
                if 1 <= t <= n_tiles:
                    turn(t - 1)
                if t >= 2:
                    gate(t - 2)

            UP = 3 * KH
            THIRDS = [range(0, UP // 3), range(UP // 3, 2 * UP // 3), range(2 * UP // 3, UP)]

            def up_pairs(m, gh, gl):
                if m < SH:
                    return three(hT_hi[:, m], hT_lo[:, m], gh, gl, KH)
                i = m % 2
                return three(xT_hi[i], xT_lo[i], gh, gl, KH)

            def up(m, pairs, part):
                if part == 0 and m >= 2:
                    pe.wait_ge(s_zmul, m - 1)
                last = product(ps_a[m % 2][:], pairs, THIRDS[part])
                if part == 2:
                    last.then_inc(s_up, 1)

            def turn_z(m):
                pe.wait_ge(s_zmul, m + 1)
                if m:
                    pe.wait_ge(s_zlo, m)
                for k in range(KI):
                    last = pe.transpose(ps_z[:, k * P:(k + 1) * P], silu[m % 2][:, k * P:(k + 1) * P], const["ident"])
                last.then_inc(s_zT, 1)

            def down(m, dh, dl):
                pe.wait_ge(s_zhi, m + 1)
                pe.wait_ge(s_zlo, m + 1)
                if 2 <= m < SH + 2:
                    pe.wait_ge(s_ysh, m - 1)
                elif m >= SH + 2:
                    pe.wait_ge(s_yex, m - SH - 1)
                product(ps_b[m % 2][:], three(zT_hi[m % 2], zT_lo[m % 2], dh, dl, KI)).then_inc(s_down, 1)

            def positions():
                pe.wait_ge(s_sel, 2)
                pe.wait_ge(s_sig, 1)
                pe.wait_ge(s_dve, 2)
                flat = sel[:].rearrange("p t e -> p (t e)")
                for t in range(n_tiles - 1):
                    n = n_tiles - 1 - t
                    pe.matmul(ps_g[:, (t + 1) * E:n_tiles * E], ones_r[:], sel[:, t:t + 1, :].broadcast_to([P, n, E]),
                              start=(t == 0), stop=False, skip_group_check=True)
                pe.matmul(ps_g[:, 0:n_tiles * E], before_r[:], flat, start=False, stop=True, skip_group_check=True)
                pe.matmul(ps_g[:, n_tiles * E:n_tiles * E + E], ones_r[:], sel_all[:], start=True, stop=True,
                          skip_group_check=True).then_inc(s_pos, 1)

            def make_list(e):
                pe.wait_ge(s_B, e + 1)
                for t in range(n_tiles):
                    last = pe.matmul(ps_g[:, 0:2 * NS], B[e % 2][:, t, :], AV[:, t, :, :, e],
                                     start=(e == 0 and t == 0), stop=(e == E - 1 and t == n_tiles - 1))
                last.then_inc(s_list, 1)

            def turn_rows(s):
                pe.wait_ge(s_gath[s % AHEAD], 16 * (s // AHEAD + 1))
                if s >= 2:
                    pe.wait_ge(s_xglo, s - 1)
                for k in range(KH):
                    last = pe.transpose(ps_t[s % 2][:, k * P:(k + 1) * P], xg[s % AHEAD][:, k * P:(k + 1) * P], const["ident"])
                last.then_inc(s_xgT, 1)

            pe.wait_ge(s_h, 2 * n_tiles)
            pe.wait_ge(s_hTlo, n_tiles)
            pe.wait_ge(s_whi, 2)
            pe.wait_ge(s_wlo, 2)
            sh_gu = (fixed(gu_hi, 1), fixed(gu_lo, 1))
            sh_d = (fixed(d_hi, 1), fixed(d_lo, 1))
            for m in range(SH):
                pairs = up_pairs(m, *sh_gu)
                up(m, pairs, 0)
                if m:
                    turn_z(m - 1)
                up(m, pairs, 1)
                if m == SH - 1:
                    turn_rows(0)
                up(m, pairs, 2)
                if m:
                    down(m - 1, *sh_d)
                if m == 0:
                    positions()
                for e in lists_after.get(m, ()):
                    make_list(e)

            pe.wait_ge(s_words, 1)
            odd_words = flag_words(pe, 1)

            def run_weights(s):
                odd = flag(odd_words, s)
                g = pe.snap(odd * (KH * 2 * I), min_val=0, max_val=KH * 2 * I)
                d = pe.snap(odd * (KI * H), min_val=0, max_val=KI * H)

                def moving(w, base, n):
                    flat = w[:].rearrange("p w k n -> p (w k n)")
                    return lambda k: flat[:, bass.ds(base + k * n, n)]

                return ((moving(gu_hi, g, 2 * I), moving(gu_lo, g, 2 * I)), (moving(d_hi, d, H), moving(d_lo, d, H)))

            d_of = {-1: sh_d}

            def slot(s, more):
                gu_w, d_of[s] = run_weights(s)
                pe.wait_ge(s_guhi, s + 1)
                pe.wait_ge(s_gulo, s + 1)
                pe.wait_ge(s_xghi, s + 1)
                pe.wait_ge(s_xglo, s + 1)
                m = SH + s
                pairs = up_pairs(m, *gu_w)
                up(m, pairs, 0)
                turn_z(m - 1)
                up(m, pairs, 1)

                def last_part():
                    up(m, pairs, 2)
                    if s:
                        pe.wait_ge(s_dhi, s)
                        pe.wait_ge(s_dlo, s)
                    down(m - 1, *d_of[s - 1])

                def then():
                    turn_rows(s + 1)
                    last_part()

                def otherwise():
                    last_part()
                    turn_z(m)
                    pe.wait_ge(s_dhi, s + 1)
                    pe.wait_ge(s_dlo, s + 1)
                    down(m, *d_of[s])
                more(then, otherwise)

            slots(pe, slot)


def kernel(x, condB_coeff, mask_Bx4096x4096_ik1, L0_cond_W, L0_cond_b, L0_ffn_gate_w, L0_ffn_bias,
           L0_ffn_Wg, L0_ffn_Wu, L0_ffn_Wd, L0_ffn_Sg, L0_ffn_Su, L0_ffn_Sd):
    import numpy as np
    import concourse.bacc as bacc
    from concourse.bass_utils import run_bass_kernel_spmd

    def rows(a):
        a = np.asarray(a)
        a = a.reshape(*a.shape[:-2], a.shape[-2] // P, P, a.shape[-1])
        return np.ascontiguousarray(np.swapaxes(a, -3, -2))

    def turned(a):
        return rows(np.swapaxes(np.asarray(a), -1, -2))

    def spread(a):
        return np.ascontiguousarray(np.broadcast_to(np.asarray(a), (P, a.shape[0])))

    def constants(E, n_tokens):
        i, n = np.arange(P), 2 * WORD_BITS
        e = np.arange(E)
        row = {
            "ident": i[:, None] == i, "before": i[:, None] < i, "ones": np.ones((P, P)), "column": i,
            "slot": np.arange(n), "power": 2.0 ** (np.arange(n) % WORD_BITS), "expert": e,
            "upto": (e[None] <= e[:, None]).ravel(), "below": (e[None] < e[:, None]).ravel(),
            "run": np.arange(E + 2), "token1": i[:, None] + 1, "trash": n_tokens + 1 + i[:, None],
        }
        return np.concatenate([np.broadcast_to(row[k], (P, w)).astype(np.float32)
                               for k, w in const_layout(E, n).items()], axis=1)

    arrays = {
        "xT": turned(x),
        "x": np.ascontiguousarray(x),
        "coeff": spread(condB_coeff),
        "mask": rows(mask_Bx4096x4096_ik1),
        "WT": turned(L0_cond_W),
        "bias_cond": spread(L0_cond_b),
        "gateT": turned(L0_ffn_gate_w),
        "bias_gate": spread(L0_ffn_bias),
        "WguT": turned(np.concatenate([np.asarray(L0_ffn_Wg), np.asarray(L0_ffn_Wu)], axis=1)),
        "WdT": turned(L0_ffn_Wd),
        "SguT": turned(np.concatenate([np.asarray(L0_ffn_Sg), np.asarray(L0_ffn_Su)], axis=0)),
        "SdT": turned(L0_ffn_Sd),
        "consts": constants(L0_ffn_gate_w.shape[0], x.shape[0] * x.shape[1]),
    }
    nc = bacc.Bacc("TRN2", target_bir_lowering=False, num_devices=1)
    args = [nc.dram_tensor(n, a.shape, mybir.dt.from_np(a.dtype), kind="ExternalInput").ap() for n, a in arrays.items()]
    out = nc.dram_tensor("out", x.shape, F32, kind="ExternalOutput").ap()
    adaln_ffn(nc, *args, out)
    r = run_bass_kernel_spmd(nc, [arrays], core_ids=[0])
    return r.results[0]["out"]
```

```python
from contextlib import ExitStack

import concourse.bass as bass
from concourse import mybir

F32 = mybir.dt.float32
F32R = mybir.dt.float32r
BF16 = mybir.dt.bfloat16
I32 = mybir.dt.int32
U32 = mybir.dt.uint32
ALU = mybir.AluOpType
ACT = mybir.ActivationFunctionType
AX_X = mybir.AxisListType.X

P = 128
LOG_P = 7
TOPK = 4
WORD_BITS = 24
AHEAD = 3
MARK = 64


def const_layout(E, n_slots):
    return {
        "ident": P, "before": P, "ones": P, "column": P, "slot": n_slots, "power": n_slots,
        "expert": E, "upto": E * E, "below": E * E, "run": E + 2, "token1": 1, "trash": 1,
    }


def adaln_ffn(nc, xT, x, coeff, mask, WT, bias_cond, gateT, bias_gate, WguT, WdT, SguT, SdT, consts, out):
    n_tiles = xT.shape[0]
    H = x.shape[2]
    KH = H // P
    E = gateT.shape[2]
    KI = WdT.shape[2]
    I = KI * P
    NT = n_tiles * P
    ROW = H + E
    MIN_SLOTS = TOPK * n_tiles
    MAX_SLOTS = MIN_SLOTS + E - 1
    NS = 2 * WORD_BITS
    assert MAX_SLOTS <= NS
    SH = n_tiles

    with ExitStack() as ctx:
        def sb(name, shape, dt=F32):
            return ctx.enter_context(nc.sbuf_tensor(name, shape, dt))

        def bank(name):
            return ctx.enter_context(nc.psum_tensor(name, [P, 512], F32))

        def sem(name):
            return ctx.enter_context(nc.semaphore(name))

        h_rows = nc.dram_tensor("h_rows", [NT, ROW], F32, kind="Internal").ap()
        sums = nc.dram_tensor("sums", [NT + P, H], F32, kind="Internal").ap()

        raw_gu = [sb(f"raw_gu{i}", [P, KH, 2 * I]) for i in range(2)]
        raw_d = [sb(f"raw_d{i}", [P, KI, H]) for i in range(2)]
        gu_hi = sb("gu_hi", [P, 2, KH, 2 * I], F32R)
        gu_lo = sb("gu_lo", [P, 2, KH, 2 * I], F32R)
        d_hi = sb("d_hi", [P, 2, KI, H], F32R)
        d_lo = sb("d_lo", [P, 2, KI, H], F32R)
        raw_mask = sb("raw_mask", [P, 2, KH * H], I32)
        sign = [sb(f"sign{i}", [P, KH, H], F32R) for i in range(2)]
        raw_xT = [sb(f"raw_xT{i}", [P, KH, P]) for i in range(2)]
        xT_hi = [sb(f"xT_hi{i}", [P, KH, P], F32R) for i in range(2)]
        xT_lo = [sb(f"xT_lo{i}", [P, KH, P], F32R) for i in range(2)]
        h_nat = [sb(f"h_nat{i}", [P, H]) for i in range(2)]
        hT_hi = sb("hT_hi", [P, n_tiles, KH, P], F32R)
        hT_lo = sb("hT_lo", [P, n_tiles, KH, P], F32R)
        b_cond = sb("b_cond", [P, H])
        c_col = sb("c_col", [P, n_tiles])
        x_nat = [t[:].rearrange("p k n -> p (k n)") for t in raw_xT]
        xg = [sb(f"xg{i}", [P, ROW]) for i in range(AHEAD)]
        silu = [sb(f"silu{i}", [P, I]) for i in range(2)]
        zT_hi = [sb(f"zT_hi{i}", [P, KI, P], F32R) for i in range(2)]
        zT_lo = [sb(f"zT_lo{i}", [P, KI, P], F32R) for i in range(2)]
        y = h_nat
        layout = const_layout(E, NS)
        k_all = sb("k_all", [P, sum(layout.values())])
        const, at = {}, 0
        for name, width in layout.items():
            const[name] = k_all[:, at:at + width]
            at += width
        before_r = sb("before_r", [P, P], F32R)
        ones_r = sb("ones_r", [P, P], F32R)
        column_b = sb("column_b", [P, P], BF16)
        slot_b = sb("slot_b", [P, NS, E], BF16)
        raw_gate = sb("raw_gate", [P, KH, E])
        gate_hi = sb("gate_hi", [P, KH, E], F32R)
        gate_lo = sb("gate_lo", [P, KH, E], F32R)
        b_gate = sb("b_gate", [P, E])
        scores = sb("scores", [P, n_tiles, E])
        top8 = sb("top8", [P, n_tiles, 8])
        idx8 = sb("idx8", [P, n_tiles, 8], U32)
        idxf = sb("idxf", [P, n_tiles, 8])
        wsum = sb("wsum", [P, n_tiles])
        winv = sb("winv", [P, n_tiles])
        wk = sb("wk", [P, n_tiles, TOPK])
        cw = sb("cw", [P, n_tiles, E])
        sel = sb("sel", [P, n_tiles, E], F32R)
        sel_all = sb("sel_all", [P, E], F32R)
        pos_i = sb("pos_i", [P, n_tiles * E], I32)
        sl_i = sb("sl_i", [P, n_tiles * E], I32)
        col_f = sb("col_f", [P, n_tiles, E])
        sl_f = sb("sl_f", [P, n_tiles, E])
        sl_b = sb("sl_b", [P, n_tiles, E], BF16)
        nt_i = sb("nt_i", [P, E], I32)
        nt_f = sb("nt_f", [P, E])
        end_f = sb("end_f", [P, E])
        base_f = sb("base_f", [P, E])
        active = sb("active", [P, E])
        active_e = sb("active_e", [P, E])
        rank = sb("rank", [P, E])
        last_run = sb("last_run", [P, 1])
        run_f = sb("run_f", [P, NS])
        run_i = sb("run_i", [1, NS], I32)
        run_odd = sb("run_odd", [1, NS], I32)
        first = sb("first", [P, NS])
        first_i = sb("first_i", [1, NS], I32)
        flags = sb("flags", [P, 2, NS])
        runs_f = sb("runs_f", [P, E + 2])
        runs_i = sb("runs_i", [1, E + 2], I32)
        words_f = sb("words_f", [P, 8])
        words = sb("words", [1, 8], I32)
        hot_e = sb("hot_e", [P, NS, E], BF16)
        AV = sb("AV", [P, n_tiles, 2, NS, E], BF16)
        found = sb("found", [P, NS])
        pad = sb("pad", [P, NS])
        take_i = sb("take_i", [P, NS], U32)
        give_i = sb("give_i", [P, NS], U32)
        cw_row = sb("cw_row", [P, E])
        cw_col = sb("cw_col", [P, MAX_SLOTS])
        scratch = raw_mask[:].rearrange("p a b -> p (a b)")
        B = [scratch[:, i * NT // 2:(i + 1) * NT // 2].bitcast(BF16).rearrange("p (t c) -> p t c", t=n_tiles)
             for i in range(2)]

        def part(start, *shape):
            n = 1
            for d in shape:
                n *= d
            v = scratch[:, start:start + n].bitcast(F32)
            if len(shape) == 2:
                return v.rearrange("p (a b) -> p a b", a=shape[0])
            return v.rearrange("p (a b c) -> p a b c", a=shape[0], b=shape[1])

        hot = part(0, n_tiles, E, TOPK)
        hotw = part(n_tiles * E * TOPK, n_tiles, E, TOPK)
        ended = part(0, NS, E)
        ended_a = part(NS * E, NS, E)
        begun = part(2 * NS * E, NS, E)
        tri = part(3 * NS * E, E, E)
        at_run = part(3 * NS * E, E + 2, E)

        ps_a = [bank(f"ps_a{i}") for i in range(2)]
        ps_b = [bank(f"ps_b{i}") for i in range(2)]
        ps_t = [bank(f"ps_t{i}") for i in range(2)]
        ps_z = bank("ps_z")
        ps_g = bank("ps_g")

        (s_small, s_wst0, s_wst1, s_whi, s_wlo, s_xhi, s_xlo, s_sign, s_cond, s_h, s_hT, s_hThi, s_hTlo,
         s_gate, s_gwhi, s_gwlo, s_sig, s_cw, s_cwst, s_sel, s_pos, s_words, s_dve, s_B, s_list, s_idx,
         s_up, s_silu, s_zmul, s_zT, s_zhi, s_zlo, s_down, s_ysh, s_yex, s_trash,
         s_guhi, s_gulo, s_dhi, s_dlo, s_xgT, s_xghi, s_xglo, s_cwsel, s_scat, s_done, s_out, s_const) = [
            sem(n) for n in (
                "small wst0 wst1 whi wlo xhi xlo sign cond h hT hThi hTlo gate gwhi gwlo sig cw cwst sel pos "
                "words dve B list idx up silu zmul zT zhi zlo down ysh yex trash guhi gulo dhi dlo xgT xghi xglo "
                "cwsel scat done out const").split()]
        s_xT = [sem(f"xT{i}") for i in range(2)]
        s_hst = [sem(f"hst{i}") for i in range(2)]
        s_mask = [sem(f"mask{i}") for i in range(2)]
        s_xnat = [sem(f"xnat{i}") for i in range(2)]
        s_yst = [sem(f"yst{i}") for i in range(2)]
        s_rawgu = [sem(f"rawgu{i}") for i in range(2)]
        s_rawd = [sem(f"rawd{i}") for i in range(2)]
        s_gath = [sem(f"gath{i}") for i in range(AHEAD)]
        N_SMALL = 5

        lists_after = {m: range(4 * (m - 1), 4 * m) for m in range(1, 5)}

        def slots(eng, inner, last):
            eng.wait_ge(s_words, 1)
            count = eng.value_load(words[0:1, 0:1], min_val=MIN_SLOTS, max_val=MAX_SLOTS)

            def step(s):
                if s + 1 < MIN_SLOTS:
                    inner(s)
                    step(s + 1)
                elif s + 1 == MAX_SLOTS:
                    last(s)
                else:
                    with eng.If(count > s + 1):
                        inner(s)
                        step(s + 1)
                    with eng.Else():
                        last(s)

            step(0)

        def flag_words(eng, kind):
            return [eng.value_load(words[0:1, 1 + 2 * kind + i:2 + 2 * kind + i], min_val=0, max_val=(1 << WORD_BITS) - 1)
                    for i in range(2)]

        def flag(pair, s):
            return (pair[s // WORD_BITS] >> (s % WORD_BITS)) & 1

        class Next:

            def __init__(self, eng):
                self.eng = eng
                eng.wait_ge(s_words, 1)
                self.word = flag_words(eng, 0)
                self.at = {}

            def look(self, s):
                run = self.eng.value_load(run_i[0:1, s:s + 1], min_val=0, max_val=E - 1)
                self.at[s] = (self.eng.snap(flag(self.word, s)), self.eng.snap(run & 1), run)

            def loads(self, s):
                return (((self.at[s][2] + 1) >> 1) + 1) * 16

            def branch(self, s, split, keep):
                is_next, odd, _ = self.at[s]
                with self.eng.If(is_next > 0):
                    with self.eng.If(odd > 0):
                        split(0)
                    with self.eng.Else():
                        split(1)
                with self.eng.Else():
                    keep()

            def split(self, s, done, counted, n, split):
                def keep():
                    self.eng.wait_ge(done, counted)
                    self.eng.sem_inc(done, n)
                self.branch(s, split, keep)

        PIECES = [slice(0, KH // 2), slice(KH // 2, KH)]

        block = ctx.enter_context(nc.Block())

        @block.sync
        def _(sp):
            def tile_in(t):
                if t >= 2:
                    sp.wait_ge(s_xhi, t - 1)
                    sp.wait_ge(s_xlo, t - 1)
                    sp.wait_ge(s_sign, t - 1)
                sp.dma_start(raw_xT[t % 2][:], xT[t]).then_inc(s_xT[t % 2], 16)
                sp.dma_start(raw_mask[:, t % 2, :], mask[t].rearrange("p k n -> p (k n)")).then_inc(s_mask[t % 2], 16)

            sp.dma_start(raw_xT[0][:], xT[0]).then_inc(s_xT[0], 16)
            sp.dma_start(raw_gu[0][:], WT).then_inc(s_wst0, 16)
            sp.dma_start(raw_mask[:, 0, :], mask[0].rearrange("p k n -> p (k n)")).then_inc(s_mask[0], 16)
            for dst, src in ((b_cond[:], bias_cond), (c_col[:], coeff), (raw_gate[:], gateT), (b_gate[:], bias_gate),
                             (k_all[:], consts)):
                sp.dma_start(dst, src).then_inc(s_small, 16)
            tile_in(1)
            for t in range(n_tiles):
                if t + 2 < n_tiles:
                    tile_in(t + 2)
                if t == 3:
                    sp.dma_start(raw_gu[1][:], SguT).then_inc(s_wst1, 16)
                    sp.dma_start(raw_d[1][:], SdT).then_inc(s_wst1, 16)
                sp.wait_ge(s_h, 2 * (t + 1))
                sp.dma_start(h_rows[t * P:(t + 1) * P, 0:H], h_nat[t % 2][:]).then_inc(s_hst[t % 2], 16)
            sp.wait_ge(s_cw, 1)
            sp.dma_start(h_rows.rearrange("(t p) c -> p t c", p=P)[:, :, H:ROW], cw[:]).then_inc(s_cwst, 16)

            def load(e1, i, raw, weights, done):
                sp.dma_start(raw[i][:], weights[bass.ds(e1 - 1, 1), :, :, :].rearrange("e p k n -> (e p) k n"))\
                    .then_inc(done[i], 16)

            def run_in(e1, i):
                load(e1, i, raw_gu, WguT, s_rawgu)
                load(e1, i, raw_d, WdT, s_rawd)

            sp.wait_ge(s_words, 1)
            sp.wait_ge(s_whi, 2)
            sp.wait_ge(s_wlo, 2)
            for r in range(2):
                run_in(sp.value_load(runs_i[0:1, r:r + 1], min_val=1, max_val=E), r)

            def next_but_one(s, i, e1):
                sp.wait_ge(s_guhi, 2 * (s + 1))
                sp.wait_ge(s_gulo, 2 * (s + 1))
                load(e1, i, raw_gu, WguT, s_rawgu)
                sp.wait_ge(s_dhi, s + 1)
                sp.wait_ge(s_dlo, s + 1)
                load(e1, i, raw_d, WdT, s_rawd)

            def slot(s):
                with sp.If(sp.value_load(first_i[0:1, s:s + 1], min_val=0, max_val=1) > 0):
                    run = sp.value_load(run_i[0:1, s:s + 1], min_val=0, max_val=E - 1)
                    e1 = sp.value_load(runs_i[0:1, bass.ds(run + 2, 1)], min_val=0, max_val=E)
                    with sp.If(e1 > 0):
                        known = sp.value_load(runs_i[0:1, bass.ds(run + 2, 1)], min_val=1, max_val=E)
                        with sp.If((run & 1) > 0):
                            next_but_one(s, 1, known)
                        with sp.Else():
                            next_but_one(s, 0, known)

            slots(sp, slot, lambda s: None)
            sp.wait_ge(s_done, 1)
            sp.dma_start(out.rearrange("t p h -> (t p) h"), sums[0:NT, :]).then_inc(s_out, 16)
            sp.wait_ge(s_out, 16)

        def gather(pool, s):
            if s >= AHEAD:
                pool.wait_ge(s_xgT, s - AHEAD + 1)
                pool.wait_ge(s_cwsel, s - AHEAD + 1)
            pool.indirect_dma_start(xg[s % AHEAD][:], None, h_rows, bass.IndirectOffsetOnAxis(ap=take_i[:, s:s + 1], axis=0))\
                .then_inc(s_gath[s % AHEAD], 16)

        @block.gpsimd
        def _(pool):
            def split_lo(s):
                pool.wait_ge((s_wst0, s_wst1)[s], 16 * (1 + s))
                pool.wait_ge(s_whi, s + 1)
                last = pool.tensor_tensor(gu_lo[:, s], raw_gu[s][:], gu_hi[:, s], ALU.subtract)
                if s:
                    last = pool.tensor_tensor(d_lo[:, s], raw_d[s][:], d_hi[:, s], ALU.subtract)
                last.then_inc(s_wlo, 1)

            split_lo(0)
            for t in range(n_tiles):
                pool.wait_ge(s_mask[t % 2], 16 * (t // 2 + 1))
                if t >= 2:
                    pool.wait_ge(s_cond, t - 1)
                pool.tensor_scalar(sign[t % 2][:], raw_mask[:, t % 2, :], 2, -1, ALU.mult, ALU.add).then_inc(s_sign, 1)
                if t == 5:
                    split_lo(1)

            pool.wait_ge(s_small, 16 * N_SMALL)
            pool.dma_start(sums[NT:NT + P, :], b_cond[:]).then_inc(s_trash, 16)

            def residual_in(m):
                pool.dma_start(x_nat[m % 2], x[m]).then_inc(s_xnat[m % 2], 16)

            pool.wait_ge(s_xhi, n_tiles)
            pool.wait_ge(s_xlo, n_tiles)
            residual_in(0)
            residual_in(1)
            for m in range(SH):
                pool.wait_ge(s_ysh, m + 1)
                pool.dma_start(sums[m * P:(m + 1) * P, :], y[m % 2][:]).then_inc(s_yst[m % 2], 16)
                if m + 2 < SH:
                    residual_in(m + 2)
                if m == SH - 3:
                    pool.wait_ge(s_idx, 1)
                    for q in s_hst:
                        pool.wait_ge(q, 16 * (n_tiles // 2))
                    pool.wait_ge(s_cwst, 16)
                    for s in range(AHEAD):
                        gather(pool, s)
            pool.wait_ge(s_trash, 16)
            for i in range(2):
                pool.wait_ge(s_yst[i], 16 * (SH // 2))

            def scatter(s):
                pool.wait_ge(s_yex, s + 1)
                if s:
                    pool.wait_ge(s_scat, 16 * s)
                pool.indirect_dma_start(sums, bass.IndirectOffsetOnAxis(ap=give_i[:, s:s + 1], axis=0), y[s % 2][:], None,
                                        compute_op=ALU.add).then_inc(s_scat, 16)

            after = Next(pool)

            def d_low(s):
                after.split(s - 1, s_dlo, s, 1, lambda i: halves(pool, i, s))

            def halves(eng, i, s):
                eng.wait_ge(s_dhi, s + 1)
                eng.tensor_tensor(d_lo[:, i], raw_d[i][:], d_hi[:, i], ALU.subtract).then_inc(s_dlo, 1)

            def inner(s):
                if AHEAD <= s + 2 < MAX_SLOTS:
                    gather(pool, s + 2)
                if s:
                    d_low(s)
                after.look(s)
                if s >= 2:
                    scatter(s - 2)

            def last(s):
                d_low(s)
                scatter(s - 2)
                scatter(s - 1)
                scatter(s)
                if s + 1 < MAX_SLOTS:
                    pool.wait_ge(s_gath[(s + 1) % AHEAD], 16 * ((s + 1) // AHEAD + 1))
                pool.wait_ge(s_scat, 16 * (s + 1))
                pool.sem_inc(s_done, 1)

            slots(pool, inner, last)

        @block.scalar
        def _(act):
            def split_hi(s):
                act.wait_ge((s_wst0, s_wst1)[s], 16 * (1 + s))
                last = act.copy(gu_hi[:, s], raw_gu[s][:])
                if s:
                    last = act.copy(d_hi[:, s], raw_d[s][:])
                last.then_inc(s_whi, 1)

            def x_hi(t):
                act.wait_ge(s_xT[t % 2], 16 * (t // 2 + 1))
                if t >= 2:
                    act.wait_ge(s_cond, t - 1)
                act.copy(xT_hi[t % 2][:], raw_xT[t % 2][:]).then_inc(s_xhi, 1)

            x_hi(0)
            split_hi(0)
            act.wait_ge(s_small, 16 * N_SMALL)
            act.copy(gate_hi[:], raw_gate[:]).then_inc(s_gwhi, 1)
            for t in range(n_tiles):
                if t + 1 < n_tiles:
                    x_hi(t + 1)
                act.wait_ge(s_hT, t + 1)
                act.copy(hT_hi[:, t], ps_t[t % 2][:]).then_inc(s_hThi, 1)
                if t == 4:
                    split_hi(1)
            act.wait_ge(s_gate, n_tiles)
            act.activation(scores[:], ps_g[:, 0:n_tiles * E], ACT.Sigmoid).then_inc(s_sig, 1)

            def silu_of(m):
                act.wait_ge(s_up, m + 1)
                if m >= 2:
                    act.wait_ge(s_zT, m - 1)
                act.activation(silu[m % 2][:], ps_a[m % 2][:, 0:I], ACT.Silu).then_inc(s_silu, 1)

            def zT_hi_of(m):
                act.wait_ge(s_zT, m + 1)
                if m >= 2:
                    act.wait_ge(s_down, m - 1)
                act.copy(zT_hi[m % 2][:], ps_z[:, 0:I]).then_inc(s_zhi, 1)

            for m in range(SH):
                silu_of(m)
                if m:
                    zT_hi_of(m - 1)
                if m == 5:
                    act.wait_ge(s_rawgu[0], 16)
                    for p in PIECES:
                        act.copy(gu_hi[:, 0, p], raw_gu[0][:, p]).then_inc(s_guhi, 1)
                    act.wait_ge(s_rawd[0], 16)
                    act.copy(d_hi[:, 0], raw_d[0][:]).then_inc(s_dhi, 1)

            def row_hi(s):
                act.wait_ge(s_xgT, s + 1)
                act.wait_ge(s_up, SH + s - 1)
                act.copy(xT_hi[s % 2][:], ps_t[s % 2][:]).then_inc(s_xghi, 1)

            def weighted(s):
                act.wait_ge(s_down, SH + s + 1)
                act.wait_ge(s_cwsel, s + 1)
                if s < 2:
                    act.wait_ge(s_yst[s % 2], 16 * (SH // 2))
                else:
                    act.wait_ge(s_scat, 16 * (s - 1))
                act.activation(y[s % 2][:], ps_b[s % 2][:], ACT.Copy, scale=cw_col[:, s:s + 1]).then_inc(s_yex, 1)

            row_hi(0)
            after = Next(act)

            def d_high(s):
                def split(i):
                    act.wait_ge(s_rawd[i], after.loads(s - 1))
                    act.wait_ge(s_down, SH + s - 1)
                    act.copy(d_hi[:, i], raw_d[i][:]).then_inc(s_dhi, 1)
                after.split(s - 1, s_dhi, s, 1, split)

            def high(s):
                def others():
                    zT_hi_of(SH + s - 1)
                    if s >= 2:
                        weighted(s - 2)

                def split(i):
                    act.wait_ge(s_rawgu[i], after.loads(s))
                    act.wait_ge(s_up, SH + s)
                    act.copy(gu_hi[:, i, PIECES[0]], raw_gu[i][:, PIECES[0]]).then_inc(s_guhi, 1)
                    others()
                    act.copy(gu_hi[:, i, PIECES[1]], raw_gu[i][:, PIECES[1]]).then_inc(s_guhi, 1)
                    row_hi(s + 1)

                def keep():
                    act.wait_ge(s_guhi, 2 * (s + 1))
                    act.sem_inc(s_guhi, 2)
                    others()
                    row_hi(s + 1)
                after.branch(s, split, keep)

            def inner(s):
                if s:
                    d_high(s)
                high(s)
                after.look(s + 1)
                silu_of(SH + s)

            def last(s):
                d_high(s)
                zT_hi_of(SH + s - 1)
                weighted(s - 2)
                silu_of(SH + s)
                weighted(s - 1)
                zT_hi_of(SH + s)
                weighted(s)

            after.look(0)
            slots(act, inner, last)

        @block.vector
        def _(dve):
            step = [0]

            def link(ins):
                step[0] += 1
                ins.then_inc(s_dve, 1)

            def linked():
                dve.wait_ge(s_dve, step[0])

            def chain(ins):
                link(ins)
                linked()

            dve.wait_ge(s_xT[0], 16)

            def x_lo(t):
                dve.wait_ge(s_xhi, t + 1)
                if t >= 2:
                    dve.wait_ge(s_cond, t - 1)
                dve.tensor_tensor(xT_lo[t % 2][:], raw_xT[t % 2][:], xT_hi[t % 2][:], ALU.subtract).then_inc(s_xlo, 1)

            x_lo(0)
            dve.wait_ge(s_gwhi, 1)
            dve.tensor_tensor(gate_lo[:], raw_gate[:], gate_hi[:], ALU.subtract).then_inc(s_gwlo, 1)
            link(dve.tensor_copy(before_r[:], const["before"]))
            link(dve.tensor_copy(ones_r[:], const["ones"]))
            link(dve.tensor_copy(column_b[:], const["column"]))
            link(dve.tensor_scalar(slot_b[:], const["slot"].unsqueeze(2).broadcast_to([P, NS, E]), float(MARK), None, ALU.add))
            for t in range(n_tiles):
                if t + 1 < n_tiles:
                    x_lo(t + 1)
                dve.wait_ge(s_cond, t + 1)
                dve.wait_ge(s_small, 16 * N_SMALL)
                if t >= 2:
                    dve.wait_ge(s_hT, t - 1)
                    dve.wait_ge(s_hst[t % 2], 16 * (t // 2))
                dve.scalar_tensor_tensor(h_nat[t % 2][:], ps_b[t % 2][:], c_col[:, t:t + 1], b_cond[:],
                                         ALU.mult, ALU.add).then_inc(s_h, 1)
                dve.wait_ge(s_h, 2 * t + 1)
                dve.tensor_tensor(h_nat[t % 2][:], h_nat[t % 2][:], ps_a[t % 2][:], ALU.add).then_inc(s_h, 1)
                dve.wait_ge(s_hThi, t + 1)
                dve.tensor_tensor(hT_lo[:, t], ps_t[t % 2][:], hT_hi[:, t], ALU.subtract).then_inc(s_hTlo, 1)

            dve.wait_ge(s_sig, 1)
            dve.wait_ge(s_sign, n_tiles)
            chain(dve.tensor_tensor(scores[:], scores[:], b_gate[:].unsqueeze(1).broadcast_to([P, n_tiles, E]), ALU.add))
            for t in range(n_tiles):
                link(dve.max(top8[:, t, :], scores[:, t, :]))
            linked()
            for t in range(n_tiles):
                link(dve.max_index(idx8[:, t, :], top8[:, t, :], scores[:, t, :]))
            link(dve.tensor_reduce(wsum[:], top8[:, :, 0:TOPK], AX_X, ALU.add))
            linked()
            link(dve.tensor_copy(idxf[:], idx8[:]))
            chain(dve.tensor_scalar(winv[:], wsum[:], 1e-20, None, ALU.add))
            for t in range(n_tiles):
                link(dve.tensor_tensor(hot[:, t], idxf[:, t, 0:TOPK].unsqueeze(1).broadcast_to([P, E, TOPK]),
                                       const["expert"].unsqueeze(2).broadcast_to([P, E, TOPK]), ALU.is_equal))
            link(dve.reciprocal(wsum[:], winv[:]))
            linked()
            with nc.allow_low_precision(reason="0 and 1"):
                dve.tensor_reduce(sel[:], hot, AX_X, ALU.add).then_inc(s_sel, 1)
            link(dve.tensor_tensor(wk[:], top8[:, :, 0:TOPK], wsum[:].unsqueeze(2).broadcast_to([P, n_tiles, TOPK]), ALU.mult))
            dve.wait_ge(s_sel, 1)
            with nc.allow_low_precision(reason="counts up to the number of tiles"):
                dve.tensor_reduce(sel_all[:], sel[:].bitcast(F32).rearrange("p t e -> p e t"), AX_X, ALU.add).then_inc(s_sel, 1)
            linked()
            for t in range(n_tiles):
                link(dve.tensor_tensor(hotw[:, t], hot[:, t], wk[:, t].unsqueeze(1).broadcast_to([P, E, TOPK]), ALU.mult))
            linked()
            dve.tensor_reduce(cw[:], hotw, AX_X, ALU.add).then_inc(s_cw, 1)
            dve.wait_ge(s_cw, 1)

            def zmul(m):
                dve.wait_ge(s_silu, m + 1)
                dve.tensor_tensor(silu[m % 2][:], silu[m % 2][:], ps_a[m % 2][:, I:2 * I], ALU.mult).then_inc(s_zmul, 1)

            def zT_lo_of(m):
                dve.wait_ge(s_zhi, m + 1)
                if m >= 2:
                    dve.wait_ge(s_down, m - 1)
                dve.tensor_tensor(zT_lo[m % 2][:], ps_z[:, 0:I], zT_hi[m % 2][:], ALU.subtract).then_inc(s_zlo, 1)

            def shared_out(m):
                dve.wait_ge(s_down, m + 1)
                dve.wait_ge(s_xnat[m % 2], 16 * (m // 2 + 1))
                dve.wait_ge(s_hst[m % 2], 16 * (n_tiles // 2))
                if m >= 2:
                    dve.wait_ge(s_yst[m % 2], 16 * (m // 2))
                dve.tensor_tensor(y[m % 2][:], x_nat[m % 2], ps_b[m % 2][:], ALU.add).then_inc(s_ysh, 1)

            def tables():
                dve.wait_ge(s_pos, 1)
                pos, counts = ps_g[:, 0:n_tiles * E], ps_g[:, n_tiles * E:n_tiles * E + E]
                link(dve.tensor_copy(pos_i[:], pos))
                chain(dve.tensor_scalar(nt_i[:], counts, float(P - 1), None, ALU.add))
                chain(dve.tensor_scalar(nt_i[:], nt_i[:], LOG_P, None, ALU.arith_shift_right))
                chain(dve.tensor_copy(nt_f[:], nt_i[:]))
                by_e = [P, E, E]
                upto = const["upto"].rearrange("p (a b) -> p a b", a=E)
                below = const["below"].rearrange("p (a b) -> p a b", a=E)
                chain(dve.tensor_tensor(tri, nt_f[:].unsqueeze(1).broadcast_to(by_e), upto, ALU.mult))
                link(dve.tensor_scalar(active[:], nt_f[:], 1.0, None, ALU.min))
                chain(dve.tensor_reduce(end_f[:], tri, AX_X, ALU.add))
                link(dve.tensor_tensor(base_f[:], end_f[:], nt_f[:], ALU.subtract))
                chain(dve.tensor_tensor(tri, active[:].unsqueeze(1).broadcast_to(by_e), below, ALU.mult))
                by_s = [P, NS, E]
                slot_of = const["slot"].unsqueeze(2).broadcast_to(by_s)
                link(dve.tensor_tensor(ended, slot_of, end_f[:].unsqueeze(1).broadcast_to(by_s), ALU.is_ge))
                chain(dve.tensor_reduce(rank[:], tri, AX_X, ALU.add))
                link(dve.tensor_tensor(ended_a, ended, active[:].unsqueeze(1).broadcast_to(by_s), ALU.mult))
                link(dve.tensor_tensor(active_e[:], active[:], const["expert"], ALU.mult))
                link(dve.tensor_tensor(begun, slot_of, base_f[:].unsqueeze(1).broadcast_to(by_s), ALU.is_ge))
                linked()
                by_r = [P, E + 2, E]
                link(dve.tensor_tensor(active_e[:], active_e[:], active[:], ALU.add))
                link(dve.tensor_reduce(run_f[:], ended_a, AX_X, ALU.add))
                link(dve.tensor_tensor(at_run, rank[:].unsqueeze(1).broadcast_to(by_r),
                                       const["run"].unsqueeze(2).broadcast_to(by_r), ALU.is_equal))
                link(dve.scalar_tensor_tensor(last_run[:], active[:, E - 1:E], -1.0, rank[:, E - 1:E], ALU.add, ALU.add))
                linked()
                link(dve.tensor_tensor(at_run, at_run, active_e[:].unsqueeze(1).broadcast_to(by_r), ALU.mult))
                link(dve.memset(first[:, 0:1], 1.0))
                link(dve.tensor_tensor(first[:, 1:NS], run_f[:, 1:NS], run_f[:, 0:NS - 1], ALU.not_equal))
                link(dve.tensor_copy(run_i[:], run_f[0:1, :]))
                linked()
                link(dve.tensor_reduce(runs_f[:], at_run, AX_X, ALU.add))
                link(dve.tensor_scalar(run_odd[:], run_i[:], 1, None, ALU.bitwise_and))
                link(dve.tensor_copy(first_i[:], first[0:1, :]))
                link(dve.tensor_scalar(flags[:, 0, :], run_f[:], last_run[:, 0:1], None, ALU.is_lt))
                linked()
                link(dve.tensor_copy(runs_i[:], runs_f[0:1, :]))
                link(dve.tensor_tensor(flags[:, 0, :], flags[:, 0, :], first[:], ALU.mult))
                link(dve.tensor_copy(flags[0:1, 1, :], run_odd[:]))
                linked()
                chain(dve.tensor_tensor(flags[0:1], flags[0:1], const["power"][0:1].unsqueeze(1).broadcast_to([1, 2, NS]), ALU.mult))
                link(dve.tensor_copy(words_f[0:1, 0:1], end_f[0:1, E - 1:E]))
                chain(dve.tensor_reduce(words_f[0:1, 1:5], flags[0:1].rearrange("p k (w b) -> p (k w) b", w=2), AX_X, ALU.add))
                dve.tensor_copy(words[0:1, 0:5], words_f[0:1, 0:5]).then_inc(s_words, 1)

            def places():
                link(dve.tensor_tensor(hot_e[:], begun, ended, ALU.subtract))
                chain(dve.tensor_scalar(sl_i[:], pos_i[:], LOG_P, None, ALU.arith_shift_right))
                link(dve.tensor_copy(sl_f[:], sl_i[:]))
                chain(dve.tensor_scalar(pos_i[:], pos_i[:], P - 1, None, ALU.bitwise_and))
                link(dve.tensor_copy(col_f[:], pos_i[:]))
                chain(dve.tensor_tensor(sl_f[:], sl_f[:], base_f[:].unsqueeze(1).broadcast_to([P, n_tiles, E]), ALU.add))
                chain(dve.scalar_tensor_tensor(sl_b[:], sel[:].bitcast(F32), float(MARK), sl_f[:], ALU.mult, ALU.add))
                for t in range(n_tiles):
                    link(dve.tensor_tensor(AV[:, t, 1], sl_b[:, t].unsqueeze(1).broadcast_to([P, NS, E]), slot_b[:], ALU.is_equal))
                linked()
                for t in range(n_tiles):
                    link(dve.tensor_scalar(AV[:, t, 0], AV[:, t, 1], const["token1"], None, ALU.mult))
                linked()
                for t in range(n_tiles):
                    link(dve.tensor_scalar(AV[:, t, 1], AV[:, t, 1], float(t), None, ALU.mult))
                linked()

            def columns(e):
                if e >= 2:
                    dve.wait_ge(s_list, e - 1)
                for t in range(n_tiles):
                    last = dve.tensor_scalar(B[e % 2][:, t, :], column_b[:], col_f[:, t, e:e + 1], None, ALU.is_equal)
                last.then_inc(s_B, 1)

            def indices():
                dve.wait_ge(s_list, E)
                chain(dve.tensor_copy(pad[:], ps_g[:, 0:NS]))
                chain(dve.scalar_tensor_tensor(found[:], ps_g[:, NS:2 * NS], float(P), pad[:], ALU.mult, ALU.add))
                link(dve.tensor_scalar(pad[:], found[:], 0.0, const["trash"], ALU.is_equal, ALU.mult))
                chain(dve.tensor_scalar(found[:], found[:], -1.0, None, ALU.add))
                link(dve.tensor_scalar(take_i[:], found[:], 0.0, None, ALU.max))
                link(dve.tensor_tensor(give_i[:], found[:], pad[:], ALU.add))
                linked()
                dve.memset(cw_row[:, 0:1], 0.0).then_inc(s_idx, 1)

            for m in range(SH):
                zmul(m)
                if m:
                    zT_lo_of(m - 1)
                    shared_out(m - 1)
                if m == 0:
                    tables()
                if m == 1:
                    places()
                if m in lists_after:
                    for e in lists_after[m]:
                        columns(e)
                if m == 4:
                    indices()
                if m == 5:
                    for n, p in enumerate(PIECES):
                        dve.wait_ge(s_guhi, n + 1)
                        dve.tensor_tensor(gu_lo[:, 0, p], raw_gu[0][:, p], gu_hi[:, 0, p], ALU.subtract).then_inc(s_gulo, 1)
                    dve.wait_ge(s_dhi, 1)
                    dve.tensor_tensor(d_lo[:, 0], raw_d[0][:], d_hi[:, 0], ALU.subtract).then_inc(s_dlo, 1)

            def row_lo(s):
                dve.wait_ge(s_gath[s % AHEAD], 16 * (s // AHEAD + 1))
                if s:
                    dve.wait_ge(s_cwsel, s)
                dve.tensor_tensor_reduce(cw_row[:], xg[s % AHEAD][:, H:ROW], hot_e[:, s, :], 1.0, 0.0, ALU.mult, ALU.add,
                                         cw_col[:, s:s + 1]).then_inc(s_cwsel, 1)
                dve.wait_ge(s_xghi, s + 1)
                dve.wait_ge(s_up, SH + s - 1)
                dve.tensor_tensor(xT_lo[s % 2][:], ps_t[s % 2][:], xT_hi[s % 2][:], ALU.subtract).then_inc(s_xglo, 1)

            row_lo(0)
            after = Next(dve)

            def low(s):
                def piece(i, n):
                    dve.wait_ge(s_guhi, 2 * (s + 1) + n + 1)
                    p = PIECES[n]
                    dve.tensor_tensor(gu_lo[:, i, p], raw_gu[i][:, p], gu_hi[:, i, p], ALU.subtract).then_inc(s_gulo, 1)

                def split(i):
                    dve.wait_ge(s_up, SH + s)
                    piece(i, 0)
                    zT_lo_of(SH + s - 1)
                    piece(i, 1)
                    row_lo(s + 1)

                def keep():
                    dve.wait_ge(s_gulo, 2 * (s + 1))
                    dve.sem_inc(s_gulo, 2)
                    zT_lo_of(SH + s - 1)
                    row_lo(s + 1)
                after.branch(s, split, keep)

            def inner(s):
                low(s)
                after.look(s + 1)
                zmul(SH + s)
                if s == 0:
                    shared_out(SH - 1)

            def last(s):
                zT_lo_of(SH + s - 1)
                zmul(SH + s)
                zT_lo_of(SH + s)

            after.look(0)
            slots(dve, inner, last)

        @block.tensor
        def _(pe):
            def product(dst, pairs, which=None):
                n = len(pairs)
                for i in which or range(n):
                    lhs, rhs = pairs[i]
                    last = pe.matmul(dst, lhs, rhs, start=(i == 0), stop=(i == n - 1))
                return last

            def three(lhi, llo, rhi, rlo, chunks):
                return [(lhs[:, k], rhs(k)) for lhs, rhs in ((lhi, rhi), (lhi, rlo), (llo, rhi)) for k in range(chunks)]

            def fixed(w, *at):
                return lambda k: w[(slice(None),) + at + (k,)]

            def cond(t):
                pe.wait_ge(s_xhi, t + 1)
                pe.wait_ge(s_xlo, t + 1)
                pe.wait_ge(s_whi, 1)
                pe.wait_ge(s_wlo, 1)
                if t >= 2:
                    pe.wait_ge(s_h, 2 * (t - 1))
                i = t % 2
                product(ps_a[i][:], three(xT_hi[i], xT_lo[i], fixed(gu_hi, 0), fixed(gu_lo, 0), KH))
                pe.wait_ge(s_sign, t + 1)
                product(ps_b[i][:], [(h[i][:, k], sign[i][:, k]) for h in (xT_hi, xT_lo) for k in range(KH)]).then_inc(s_cond, 1)

            def turn(t):
                pe.wait_ge(s_h, 2 * (t + 1))
                pe.wait_ge(s_small, 16 * N_SMALL)
                if t >= 2:
                    pe.wait_ge(s_hTlo, t - 1)
                for k in range(KH):
                    last = pe.transpose(ps_t[t % 2][:, k * P:(k + 1) * P], h_nat[t % 2][:, k * P:(k + 1) * P], const["ident"])
                last.then_inc(s_hT, 1)

            def gate(t):
                pe.wait_ge(s_hThi, t + 1)
                pe.wait_ge(s_hTlo, t + 1)
                pe.wait_ge(s_gwlo, 1)
                product(ps_g[:, t * E:(t + 1) * E], three(hT_hi[:, t], hT_lo[:, t], fixed(gate_hi), fixed(gate_lo), KH))\
                    .then_inc(s_gate, 1)

            for t in range(n_tiles + 2):
                if t < n_tiles:
                    cond(t)
                if 1 <= t <= n_tiles:
                    turn(t - 1)
                if t >= 2:
                    gate(t - 2)

            UP = 3 * KH
            THIRDS = [range(0, UP // 3), range(UP // 3, 2 * UP // 3), range(2 * UP // 3, UP)]

            def up_pairs(m, gh, gl):
                if m < SH:
                    return three(hT_hi[:, m], hT_lo[:, m], gh, gl, KH)
                i = m % 2
                return three(xT_hi[i], xT_lo[i], gh, gl, KH)

            def up(m, pairs, part):
                if part == 0 and m >= 2:
                    pe.wait_ge(s_zmul, m - 1)
                last = product(ps_a[m % 2][:], pairs, THIRDS[part])
                if part == 2:
                    last.then_inc(s_up, 1)

            def turn_z(m):
                pe.wait_ge(s_zmul, m + 1)
                if m:
                    pe.wait_ge(s_zlo, m)
                for k in range(KI):
                    last = pe.transpose(ps_z[:, k * P:(k + 1) * P], silu[m % 2][:, k * P:(k + 1) * P], const["ident"])
                last.then_inc(s_zT, 1)

            def down(m, dh, dl):
                s = m - SH
                pe.wait_ge(s_zhi, m + 1)
                if s >= 0:
                    pe.wait_ge(s_dhi, s + 1)
                if 2 <= m < SH + 2:
                    pe.wait_ge(s_ysh, m - 1)
                elif m >= SH + 2:
                    pe.wait_ge(s_yex, m - SH - 1)
                pairs = three(zT_hi[m % 2], zT_lo[m % 2], dh, dl, KI)
                product(ps_b[m % 2][:], pairs, range(0, KI))
                if s >= 0:
                    pe.wait_ge(s_dlo, s + 1)
                product(ps_b[m % 2][:], pairs, range(KI, 2 * KI))
                pe.wait_ge(s_zlo, m + 1)
                product(ps_b[m % 2][:], pairs, range(2 * KI, 3 * KI)).then_inc(s_down, 1)

            def positions():
                pe.wait_ge(s_sel, 2)
                pe.wait_ge(s_sig, 1)
                pe.wait_ge(s_dve, 2)
                flat = sel[:].rearrange("p t e -> p (t e)")
                for t in range(n_tiles - 1):
                    n = n_tiles - 1 - t
                    pe.matmul(ps_g[:, (t + 1) * E:n_tiles * E], ones_r[:], sel[:, t:t + 1, :].broadcast_to([P, n, E]),
                              start=(t == 0), stop=False, skip_group_check=True)
                pe.matmul(ps_g[:, 0:n_tiles * E], before_r[:], flat, start=False, stop=True, skip_group_check=True)
                pe.matmul(ps_g[:, n_tiles * E:n_tiles * E + E], ones_r[:], sel_all[:], start=True, stop=True,
                          skip_group_check=True).then_inc(s_pos, 1)

            def make_list(e):
                pe.wait_ge(s_B, e + 1)
                for t in range(n_tiles):
                    last = pe.matmul(ps_g[:, 0:2 * NS], B[e % 2][:, t, :], AV[:, t, :, :, e],
                                     start=(e == 0 and t == 0), stop=(e == E - 1 and t == n_tiles - 1))
                last.then_inc(s_list, 1)

            def turn_rows(s):
                pe.wait_ge(s_gath[s % AHEAD], 16 * (s // AHEAD + 1))
                if s >= 2:
                    pe.wait_ge(s_xglo, s - 1)
                for k in range(KH):
                    last = pe.transpose(ps_t[s % 2][:, k * P:(k + 1) * P], xg[s % AHEAD][:, k * P:(k + 1) * P], const["ident"])
                last.then_inc(s_xgT, 1)

            pe.wait_ge(s_h, 2 * n_tiles)
            pe.wait_ge(s_hTlo, n_tiles)
            pe.wait_ge(s_whi, 2)
            pe.wait_ge(s_wlo, 2)
            sh_gu = (fixed(gu_hi, 1), fixed(gu_lo, 1))
            sh_d = (fixed(d_hi, 1), fixed(d_lo, 1))
            for m in range(SH):
                pairs = up_pairs(m, *sh_gu)
                up(m, pairs, 0)
                if m:
                    turn_z(m - 1)
                up(m, pairs, 1)
                if m == SH - 1:
                    turn_rows(0)
                up(m, pairs, 2)
                if m:
                    down(m - 1, *sh_d)
                if m == 0:
                    positions()
                for e in lists_after.get(m, ()):
                    make_list(e)

            pe.wait_ge(s_words, 1)
            odd_words = flag_words(pe, 1)

            def run_weights(s):
                odd = flag(odd_words, s)
                g = pe.snap(odd * (KH * 2 * I), min_val=0, max_val=KH * 2 * I)
                d = pe.snap(odd * (KI * H), min_val=0, max_val=KI * H)

                def moving(w, base, n):
                    flat = w[:].rearrange("p w k n -> p (w k n)")
                    return lambda k: flat[:, bass.ds(base + k * n, n)]

                return ((moving(gu_hi, g, 2 * I), moving(gu_lo, g, 2 * I)), (moving(d_hi, d, H), moving(d_lo, d, H)))

            d_of = {-1: sh_d}

            def begin(s):
                gu_w, d_of[s] = run_weights(s)
                m = SH + s
                pairs = up_pairs(m, *gu_w)
                pe.wait_ge(s_guhi, 2 * (s + 1))
                pe.wait_ge(s_xghi, s + 1)
                up(m, pairs, 0)
                turn_z(m - 1)
                pe.wait_ge(s_gulo, 2 * (s + 1))
                up(m, pairs, 1)

                def finish():
                    pe.wait_ge(s_xglo, s + 1)
                    up(m, pairs, 2)
                    down(m - 1, *d_of[s - 1])
                return finish

            def inner(s):
                finish = begin(s)
                turn_rows(s + 1)
                finish()

            def last(s):
                begin(s)()
                turn_z(SH + s)
                down(SH + s, *d_of[s])

            slots(pe, inner, last)


def kernel(x, condB_coeff, mask_Bx4096x4096_ik1, L0_cond_W, L0_cond_b, L0_ffn_gate_w, L0_ffn_bias,
           L0_ffn_Wg, L0_ffn_Wu, L0_ffn_Wd, L0_ffn_Sg, L0_ffn_Su, L0_ffn_Sd):
    import numpy as np
    import concourse.bacc as bacc
    from concourse.bass_utils import run_bass_kernel_spmd

    def rows(a):
        a = np.asarray(a)
        a = a.reshape(*a.shape[:-2], a.shape[-2] // P, P, a.shape[-1])
        return np.ascontiguousarray(np.swapaxes(a, -3, -2))

    def turned(a):
        return rows(np.swapaxes(np.asarray(a), -1, -2))

    def spread(a):
        return np.ascontiguousarray(np.broadcast_to(np.asarray(a), (P, a.shape[0])))

    def constants(E, n_tokens):
        i, n = np.arange(P), 2 * WORD_BITS
        e = np.arange(E)
        row = {
            "ident": i[:, None] == i, "before": i[:, None] < i, "ones": np.ones((P, P)), "column": i,
            "slot": np.arange(n), "power": 2.0 ** (np.arange(n) % WORD_BITS), "expert": e,
            "upto": (e[None] <= e[:, None]).ravel(), "below": (e[None] < e[:, None]).ravel(),
            "run": np.arange(E + 2), "token1": i[:, None] + 1, "trash": n_tokens + 1 + i[:, None],
        }
        return np.concatenate([np.broadcast_to(row[k], (P, w)).astype(np.float32)
                               for k, w in const_layout(E, n).items()], axis=1)

    arrays = {
        "xT": turned(x),
        "x": np.ascontiguousarray(x),
        "coeff": spread(condB_coeff),
        "mask": rows(mask_Bx4096x4096_ik1),
        "WT": turned(L0_cond_W),
        "bias_cond": spread(L0_cond_b),
        "gateT": turned(L0_ffn_gate_w),
        "bias_gate": spread(L0_ffn_bias),
        "WguT": turned(np.concatenate([np.asarray(L0_ffn_Wg), np.asarray(L0_ffn_Wu)], axis=1)),
        "WdT": turned(L0_ffn_Wd),
        "SguT": turned(np.concatenate([np.asarray(L0_ffn_Sg), np.asarray(L0_ffn_Su)], axis=0)),
        "SdT": turned(L0_ffn_Sd),
        "consts": constants(L0_ffn_gate_w.shape[0], x.shape[0] * x.shape[1]),
    }
    nc = bacc.Bacc("TRN2", target_bir_lowering=False, num_devices=1)
    args = [nc.dram_tensor(n, a.shape, mybir.dt.from_np(a.dtype), kind="ExternalInput").ap() for n, a in arrays.items()]
    out = nc.dram_tensor("out", x.shape, F32, kind="ExternalOutput").ap()
    adaln_ffn(nc, *args, out)
    r = run_bass_kernel_spmd(nc, [arrays], core_ids=[0])
    return r.results[0]["out"]
```

```python
from contextlib import ExitStack

import concourse.bass as bass
from concourse import mybir

F32 = mybir.dt.float32
F32R = mybir.dt.float32r
BF16 = mybir.dt.bfloat16
I32 = mybir.dt.int32
U32 = mybir.dt.uint32
ALU = mybir.AluOpType
ACT = mybir.ActivationFunctionType
AX_X = mybir.AxisListType.X

P = 128
LOG_P = 7
TOPK = 4
WORD_BITS = 24
AHEAD = 3
PAIR = 2
MARK = 64


def const_layout(E, n_slots):
    return {
        "ident": P, "before": P, "ones": P, "column": P, "slot": n_slots, "power": n_slots,
        "expert": E, "upto": E * E, "below": E * E, "run": E + 2, "token1": 1, "trash": 1,
    }


def adaln_ffn(nc, xT, x, coeff, mask, WT, bias_cond, gateT, bias_gate, WguT, WdT, SguT, SdT, consts, out):
    n_tiles = xT.shape[0]
    H = x.shape[2]
    KH = H // P
    E = gateT.shape[2]
    KI = WdT.shape[2]
    I = KI * P
    NT = n_tiles * P
    ROW = H + E
    MIN_SLOTS = TOPK * n_tiles
    MAX_SLOTS = MIN_SLOTS + E - 1
    NS = 2 * WORD_BITS
    assert MAX_SLOTS <= NS
    SH = n_tiles

    with ExitStack() as ctx:
        def sb(name, shape, dt=F32):
            return ctx.enter_context(nc.sbuf_tensor(name, shape, dt))

        def bank(name):
            return ctx.enter_context(nc.psum_tensor(name, [P, 512], F32))

        def sem(name):
            return ctx.enter_context(nc.semaphore(name))

        h_rows = nc.dram_tensor("h_rows", [NT, ROW], F32, kind="Internal").ap()

        raw_gu = [sb(f"raw_gu{i}", [P, KH, 2 * I]) for i in range(2)]
        raw_d = [sb(f"raw_d{i}", [P, KI, H]) for i in range(2)]
        gu_hi = sb("gu_hi", [P, 2, KH, 2 * I], F32R)
        gu_lo = sb("gu_lo", [P, 2, KH, 2 * I], F32R)
        d_hi = sb("d_hi", [P, 2, KI, H], F32R)
        d_lo = sb("d_lo", [P, 2, KI, H], F32R)
        raw_mask = sb("raw_mask", [P, 2, KH * H], I32)
        sign = [sb(f"sign{i}", [P, KH, H], F32R) for i in range(2)]
        raw_xT = [sb(f"raw_xT{i}", [P, KH, P]) for i in range(2)]
        xT_hi = [sb(f"xT_hi{i}", [P, KH, P], F32R) for i in range(2)]
        xT_lo = [sb(f"xT_lo{i}", [P, KH, P], F32R) for i in range(2)]
        h_nat = [sb(f"h_nat{i}", [P, H]) for i in range(2)]
        hT_hi = sb("hT_hi", [P, n_tiles, KH, P], F32R)
        hT_lo = sb("hT_lo", [P, n_tiles, KH, P], F32R)
        b_cond = sb("b_cond", [P, H])
        c_col = sb("c_col", [P, n_tiles])
        x_nat = [t[:].rearrange("p k n -> p (k n)") for t in raw_xT]
        xg = [sb(f"xg{i}", [P, ROW]) for i in range(AHEAD)]
        silu = [sb(f"silu{i}", [P, I]) for i in range(2)]
        zT_hi = [sb(f"zT_hi{i}", [P, KI, P], F32R) for i in range(2)]
        zT_lo = [sb(f"zT_lo{i}", [P, KI, P], F32R) for i in range(2)]
        y = h_nat
        layout = const_layout(E, NS)
        k_all = sb("k_all", [P, sum(layout.values())])
        const, at = {}, 0
        for name, width in layout.items():
            const[name] = k_all[:, at:at + width]
            at += width
        before_r = sb("before_r", [P, P], F32R)
        ones_r = sb("ones_r", [P, P], F32R)
        column_b = sb("column_b", [P, P, n_tiles], BF16)
        slot_b = sb("slot_b", [P, NS, E], BF16)
        raw_gate = sb("raw_gate", [P, KH, E])
        gate_hi = sb("gate_hi", [P, KH, E], F32R)
        gate_lo = sb("gate_lo", [P, KH, E], F32R)
        b_gate = sb("b_gate", [P, E])
        scores = sb("scores", [P, n_tiles, E])
        top8 = sb("top8", [P, n_tiles, 8])
        idx8 = sb("idx8", [P, n_tiles, 8], U32)
        idxf = sb("idxf", [P, PAIR, 8])
        hot = sb("hot", [P, PAIR, E, TOPK])
        wsum = sb("wsum", [P, n_tiles])
        winv = sb("winv", [P, n_tiles])
        cw = sb("cw", [P, n_tiles, E])
        sel = sb("sel", [P, n_tiles, E], F32R)
        sel_all = sb("sel_all", [P, E], F32R)
        pos_i = sb("pos_i", [P, n_tiles * E], I32)
        sl_i = sb("sl_i", [P, n_tiles * E], I32)
        col_b = sb("col_b", [P, E, n_tiles], BF16)
        sl_f = sb("sl_f", [P, n_tiles, E])
        sl_b = sb("sl_b", [P, n_tiles, E], BF16)
        nt_i = sb("nt_i", [P, E], I32)
        nt_f = sb("nt_f", [P, E])
        end_f = sb("end_f", [P, E])
        base_f = sb("base_f", [P, E])
        active = sb("active", [P, E])
        active_b = sb("active_b", [P, E], BF16)
        ends = sb("ends", [P, E], BF16)
        bases = sb("bases", [P, E], BF16)
        active_e = sb("active_e", [P, E])
        rank = sb("rank", [P, E])
        last_run = sb("last_run", [P, 1])
        run_f = sb("run_f", [P, NS])
        run_i = sb("run_i", [1, NS], I32)
        run_odd = sb("run_odd", [1, NS], I32)
        first = sb("first", [P, NS])
        first_i = sb("first_i", [1, NS], I32)
        runs_f = sb("runs_f", [P, E + 2])
        runs_i = sb("runs_i", [1, E + 2], I32)
        words_f = sb("words_f", [P, 8])
        words = sb("words", [1, 8], I32)
        AV = sb("AV", [P, n_tiles, 2, NS, E], BF16)
        found = sb("found", [P, NS])
        pad = sb("pad", [P, NS])
        take_i = sb("take_i", [P, NS], U32)
        give_i = sb("give_i", [P, NS], U32)
        cw_row = sb("cw_row", [P, E])
        cw_col = sb("cw_col", [P, MAX_SLOTS])
        scratch = raw_mask[:].rearrange("p a b -> p (a b)")
        def part(start, *shape):
            n = 1
            for d in shape:
                n *= d
            v = scratch[:, start:start + n].bitcast(F32)
            return v.rearrange("p (a b) -> p a b", a=shape[0])

        ended, ended_a, begun = [
            scratch[:, i * NS * E:i * NS * E + NS * E // 2].bitcast(BF16).rearrange("p (s e) -> p s e", e=E) for i in range(3)]
        tri = part(3 * NS * E, E, E)
        at_run = part(3 * NS * E, E + 2, E)
        at = 3 * NS * E + (E + 2) * E
        B = [scratch[:, at + i * NT // 2:at + (i + 1) * NT // 2].bitcast(BF16).rearrange("p (c t) -> p c t", t=n_tiles)
             for i in range(2)]

        at += NT
        hot_e = scratch[:, at:at + NS * E // 2].bitcast(BF16).rearrange("p (s e) -> p s e", e=E)
        flags = part(at + NS * E // 2, 2, NS)

        ps_a = [bank(f"ps_a{i}") for i in range(2)]
        ps_b = [bank(f"ps_b{i}") for i in range(2)]
        ps_t = [bank(f"ps_t{i}") for i in range(2)]
        ps_z = bank("ps_z")
        ps_g = bank("ps_g")
        ps_gate = [ps_g, ps_z]

        PIECES = [slice(0, KH // 2), slice(KH // 2, KH)]
        (s_small, s_whi, s_wlo, s_xhi, s_xlo, s_sign, s_cond, s_h, s_hT, s_hThi, s_hTlo,
         s_gate, s_gwhi, s_gwlo, s_sig, s_cw, s_cwst, s_sel, s_pos, s_words, s_dve, s_B, s_list, s_idx,
         s_up, s_silu, s_zmul, s_zT, s_zhi, s_zlo, s_down, s_ysh, s_ycopy, s_yex, s_trash,
         s_guhi, s_gulo, s_dhi, s_dlo, s_xgT, s_xghi, s_xglo, s_cwsel, s_scat, s_done, s_bias, s_eq, s_av, s_avp, s_firstlo,
         s_ranked, s_hot) = [
            sem(n) for n in (
                "small whi wlo xhi xlo sign cond h hT hThi hTlo gate gwhi gwlo sig cw cwst sel pos "
                "words dve B list idx up silu zmul zT zhi zlo down ysh ycopy yex trash guhi gulo dhi dlo xgT xghi xglo "
                "cwsel scat done bias eq av avp firstlo ranked hot").split()]
        s_w = [sem(f"w{i}") for i in range(len(PIECES))]
        s_sw = [sem(f"sw{i}") for i in range(len(PIECES) + 1)]
        s_xT = [sem(f"xT{i}") for i in range(2)]
        s_hst = [sem(f"hst{i}") for i in range(2)]
        s_mask = [sem(f"mask{i}") for i in range(2)]
        s_xnat = [sem(f"xnat{i}") for i in range(2)]
        s_yst = [sem(f"yst{i}") for i in range(2)]
        s_rawgu = [sem(f"rawgu{i}") for i in range(2)]
        s_rawd = [sem(f"rawd{i}") for i in range(2)]
        s_gath = [sem(f"gath{i}") for i in range(AHEAD)]
        N_SMALL = 3
        N_SPLIT = 5

        SPLIT_SHARED = {3: [0], 5: [1, 2]}
        SPLIT_AT = SH - 2

        ACT_AV = {1: [0, 1], 2: [2, 3, 4]}
        POOL_AV = [n_tiles - 1]

        lists_after = {3: range(0, 2), 4: range(2, 4), 5: range(4, 10), 6: range(10, E)}

        def slots_in_use(eng):
            eng.wait_ge(s_words, 1)
            return eng.value_load(words[0:1, 0:1], min_val=MIN_SLOTS, max_val=MAX_SLOTS)

        def slots(eng, inner, last, count=None):
            if count is None:
                count = slots_in_use(eng)

            def step(s):
                if s + 1 < MIN_SLOTS:
                    inner(s)
                    step(s + 1)
                elif s + 1 == MAX_SLOTS:
                    last(s)
                else:
                    with eng.If(count > s + 1):
                        inner(s)
                        step(s + 1)
                    with eng.Else():
                        last(s)

            step(0)

        def flag_words(eng, kind):
            return [eng.value_load(words[0:1, 1 + 2 * kind + i:2 + 2 * kind + i], min_val=0, max_val=(1 << WORD_BITS) - 1)
                    for i in range(2)]

        def flag(pair, s):
            return (pair[s // WORD_BITS] >> (s % WORD_BITS)) & 1

        class Next:

            def __init__(self, eng):
                self.eng = eng
                eng.wait_ge(s_words, 1)
                self.word = flag_words(eng, 0)
                self.at = {}

            def look(self, s):
                run = self.eng.value_load(run_i[0:1, s:s + 1], min_val=0, max_val=E - 1)
                self.at[s] = (self.eng.snap(flag(self.word, s)), self.eng.snap(run & 1), run)

            def loads(self, s):
                return (((self.at[s][2] + 1) >> 1) + 1) * 16

            def branch(self, s, split, keep):
                is_next, odd, _ = self.at[s]
                with self.eng.If(is_next > 0):
                    with self.eng.If(odd > 0):
                        split(0)
                    with self.eng.Else():
                        split(1)
                with self.eng.Else():
                    keep()

            def split(self, s, done, counted, n, split):
                def keep():
                    self.eng.wait_ge(done, counted)
                    self.eng.sem_inc(done, n)
                self.branch(s, split, keep)

        block = ctx.enter_context(nc.Block())

        @block.sync
        def _(sp):
            def tile_in(t):
                if t >= 2:
                    sp.wait_ge(s_xhi, t - 1)
                    sp.wait_ge(s_xlo, t - 1)
                    sp.wait_ge(s_sign, t - 1)
                sp.dma_start(raw_xT[t % 2][:], xT[t]).then_inc(s_xT[t % 2], 16)
                sp.dma_start(raw_mask[:, t % 2, :], mask[t].rearrange("p k n -> p (k n)")).then_inc(s_mask[t % 2], 16)

            sp.dma_start(raw_xT[0][:], xT[0]).then_inc(s_xT[0], 16)
            for p, done in zip(PIECES, s_w):
                sp.dma_start(raw_gu[0][:, p], WT[:, p]).then_inc(done, 16)
            sp.dma_start(raw_mask[:, 0, :], mask[0].rearrange("p k n -> p (k n)")).then_inc(s_mask[0], 16)
            sp.dma_start(b_cond[:], bias_cond).then_inc(s_bias, 16)
            sp.dma_start(c_col[:], coeff).then_inc(s_bias, 16)
            tile_in(1)
            for dst, src in ((raw_gate[:], gateT), (b_gate[:], bias_gate), (k_all[:], consts)):
                sp.dma_start(dst, src).then_inc(s_small, 16)
            for t in range(n_tiles):
                if t + 2 < n_tiles:
                    tile_in(t + 2)
                if t in (1, 2):
                    p = PIECES[t - 1]
                    sp.dma_start(raw_gu[1][:, p], SguT[:, p]).then_inc(s_sw[t - 1], 16)
                if t == 3:
                    sp.dma_start(raw_d[1][:], SdT).then_inc(s_sw[2], 16)
                sp.wait_ge(s_h, 2 * (t + 1))
                sp.dma_start(h_rows[t * P:(t + 1) * P, 0:H], h_nat[t % 2][:]).then_inc(s_hst[t % 2], 16)
            sp.wait_ge(s_cw, n_tiles)
            sp.dma_start(h_rows.rearrange("(t p) c -> p t c", p=P)[:, :, H:ROW], cw[:]).then_inc(s_cwst, 16)

            def load(e1, i, raw, weights, done):
                sp.dma_start(raw[i][:], weights[bass.ds(e1 - 1, 1), :, :, :].rearrange("e p k n -> (e p) k n"))\
                    .then_inc(done[i], 16)

            def run_in(e1, i):
                load(e1, i, raw_gu, WguT, s_rawgu)
                load(e1, i, raw_d, WdT, s_rawd)

            def residual_in(m):
                sp.dma_start(x_nat[m % 2], x[m]).then_inc(s_xnat[m % 2], 16)

            def rows_out(m):
                sp.wait_ge(s_ysh, m + 1)
                sp.dma_start(out[m * P:(m + 1) * P, :], y[m % 2][:]).then_inc(s_yst[m % 2], 16)
                if m + 2 < SH:
                    residual_in(m + 2)

            sp.dma_start(out[NT:NT + P, :], b_cond[:]).then_inc(s_trash, 16)
            sp.wait_ge(s_xhi, n_tiles)
            sp.wait_ge(s_xlo, n_tiles)
            residual_in(0)
            residual_in(1)
            for m in range(3):
                rows_out(m)
            sp.wait_ge(s_words, 1)
            sp.wait_ge(s_whi, N_SPLIT)
            sp.wait_ge(s_wlo, N_SPLIT)
            for r in range(2):
                run_in(sp.value_load(runs_i[0:1, r:r + 1], min_val=1, max_val=E), r)
            rows_out(3)
            rows_out(4)

            def next_but_one(s, i, e1):
                sp.wait_ge(s_guhi, 2 * (s + 1))
                sp.wait_ge(s_gulo, 2 * (s + 1))
                if s == 0:
                    sp.wait_ge(s_firstlo, 1)
                load(e1, i, raw_gu, WguT, s_rawgu)
                sp.wait_ge(s_dhi, s + 1)
                sp.wait_ge(s_dlo, s + 1)
                load(e1, i, raw_d, WdT, s_rawd)

            def slot(s):
                with sp.If(sp.value_load(first_i[0:1, s:s + 1], min_val=0, max_val=1) > 0):
                    run = sp.value_load(run_i[0:1, s:s + 1], min_val=0, max_val=E - 1)
                    e1 = sp.value_load(runs_i[0:1, bass.ds(run + 2, 1)], min_val=0, max_val=E)
                    with sp.If(e1 > 0):
                        known = sp.value_load(runs_i[0:1, bass.ds(run + 2, 1)], min_val=1, max_val=E)
                        with sp.If((run & 1) > 0):
                            next_but_one(s, 1, known)
                        with sp.Else():
                            next_but_one(s, 0, known)

            def inner(s):
                slot(s)
                if s == 0:
                    for m in range(5, SH - 1):
                        rows_out(m)
                if s == 1:
                    rows_out(SH - 1)

            slots(sp, inner, lambda s: None)
            sp.wait_ge(s_done, 1)

        def shared_piece(n):
            if n < len(PIECES):
                return tuple(w[:, 1, PIECES[n]] for w in (gu_lo, gu_hi)) + (raw_gu[1][:, PIECES[n]],)
            return d_lo[:, 1], d_hi[:, 1], raw_d[1][:]

        def first_run_low(eng, n, done, by):
            eng.wait_ge(s_guhi, n + 1)
            p = PIECES[n]
            eng.tensor_tensor(gu_lo[:, 0, p], raw_gu[0][:, p], gu_hi[:, 0, p], ALU.subtract).then_inc(done, by)

        def gather(pool, s):
            if s >= AHEAD:
                pool.wait_ge(s_xgT, s - AHEAD + 1)
                pool.wait_ge(s_cwsel, s - AHEAD + 1)
            pool.indirect_dma_start(xg[s % AHEAD][:], None, h_rows, bass.IndirectOffsetOnAxis(ap=take_i[:, s:s + 1], axis=0))\
                .then_inc(s_gath[s % AHEAD], 16)

        @block.gpsimd
        def _(pool):
            for t in range(n_tiles):
                pool.wait_ge(s_mask[t % 2], 16 * (t // 2 + 1))
                if t >= 2:
                    pool.wait_ge(s_cond, t - 1)
                pool.tensor_scalar(sign[t % 2][:], raw_mask[:, t % 2, :], 2, -1, ALU.mult, ALU.add).then_inc(s_sign, 1)

            def add_x(m):
                pool.wait_ge(s_ycopy, m + 1)
                pool.wait_ge(s_xnat[m % 2], 16 * (m // 2 + 1))
                pool.tensor_tensor(y[m % 2][:], y[m % 2][:], x_nat[m % 2], ALU.add).then_inc(s_ysh, 1)

            def experts_of_slots():
                pool.wait_ge(s_ranked, 2)
                pool.tensor_tensor(hot_e, begun, ended, ALU.subtract).then_inc(s_hot, 1)

            pool.wait_ge(s_small, 16 * N_SMALL)
            for t in POOL_AV:
                pool.wait_ge(s_eq, t + 1)
                pool.tensor_scalar(AV[:, t, 0], AV[:, t, 1], const["token1"], None, ALU.mult).then_inc(s_avp, 1)
            add_x(0)
            add_x(1)
            experts_of_slots()
            for m in range(2, SH - 3):
                add_x(m)
            first_run_low(pool, 0, s_firstlo, 1)
            pool.wait_ge(s_idx, 2)
            for q in s_hst:
                pool.wait_ge(q, 16 * (n_tiles // 2))
            pool.wait_ge(s_cwst, 16)
            for s in range(AHEAD):
                gather(pool, s)
            pool.wait_ge(s_dhi, 1)
            pool.tensor_tensor(d_lo[:, 0], raw_d[0][:], d_hi[:, 0], ALU.subtract).then_inc(s_dlo, 1)
            for m in range(SH - 3, SH - 1):
                add_x(m)

            def scatter(s):
                pool.wait_ge(s_yex, s + 1)
                if s == 0:
                    pool.wait_ge(s_trash, 16)
                    for i in range(2):
                        pool.wait_ge(s_yst[i], 16 * (SH // 2))
                if s:
                    pool.wait_ge(s_scat, 16 * s)
                pool.indirect_dma_start(out, bass.IndirectOffsetOnAxis(ap=give_i[:, s:s + 1], axis=0), y[s % 2][:], None,
                                        compute_op=ALU.add).then_inc(s_scat, 16)

            after = Next(pool)

            def d_low(s):
                def split(i):
                    pool.wait_ge(s_dhi, s + 1)
                    pool.tensor_tensor(d_lo[:, i], raw_d[i][:], d_hi[:, i], ALU.subtract).then_inc(s_dlo, 1)
                after.split(s - 1, s_dlo, s, 1, split)

            def inner(s):
                if AHEAD <= s + AHEAD - 1 < MAX_SLOTS:
                    gather(pool, s + AHEAD - 1)
                if s == 1:
                    add_x(SH - 1)
                if s:
                    d_low(s)
                after.look(s)
                if s >= 2:
                    scatter(s - 2)

            def last(s):
                d_low(s)
                scatter(s - 2)
                scatter(s - 1)
                scatter(s)
                if s + 1 < MAX_SLOTS:
                    pool.wait_ge(s_gath[(s + 1) % AHEAD], 16 * ((s + 1) // AHEAD + 1))
                pool.wait_ge(s_scat, 16 * (s + 1))
                pool.sem_inc(s_done, 1)

            slots(pool, inner, last)

        @block.scalar
        def _(act):
            def high_of(dst, src):
                act.copy(dst, src).then_inc(s_whi, 1)

            def x_hi(t):
                if t >= n_tiles:
                    return
                act.wait_ge(s_xT[t % 2], 16 * (t // 2 + 1))
                if t >= 2:
                    act.wait_ge(s_cond, t - 1)
                act.copy(xT_hi[t % 2][:], raw_xT[t % 2][:]).then_inc(s_xhi, 1)

            x_hi(0)
            for p, done in zip(PIECES, s_w):
                act.wait_ge(done, 16)
                high_of(gu_hi[:, 0, p], raw_gu[0][:, p])
            x_hi(1)
            act.wait_ge(s_small, 16 * N_SMALL)
            act.copy(gate_hi[:], raw_gate[:]).then_inc(s_gwhi, 1)
            for t in range(n_tiles + 1):
                x_hi(t + 2)
                if t:
                    act.wait_ge(s_hT, t)
                    act.copy(hT_hi[:, t - 1], ps_t[(t - 1) % 2][:]).then_inc(s_hThi, 1)
                for n in SPLIT_SHARED.get(t, ()):
                    act.wait_ge(s_sw[n], 16)
                    _, high, raw = shared_piece(n)
                    high_of(high, raw)
                if t >= PAIR + 1 and t % PAIR or t == n_tiles:
                    j = (t - PAIR) // PAIR
                    act.wait_ge(s_gate, PAIR * (j + 1))
                    at = slice(PAIR * j, PAIR * (j + 1))
                    act.activation(scores[:, at], ps_gate[j % 2][:, at.start * E:at.stop * E], ACT.Sigmoid).then_inc(s_sig, 1)

            def silu_of(m):
                act.wait_ge(s_up, m + 1)
                if m >= 2:
                    act.wait_ge(s_zT, m - 1)
                act.activation(silu[m % 2][:], ps_a[m % 2][:, 0:I], ACT.Silu).then_inc(s_silu, 1)

            def zT_hi_of(m):
                act.wait_ge(s_zT, m + 1)
                if m >= 2:
                    act.wait_ge(s_down, m - 1)
                act.copy(zT_hi[m % 2][:], ps_z[:, 0:I]).then_inc(s_zhi, 1)

            def share_out(m):
                act.wait_ge(s_down, m + 1)
                act.wait_ge(s_hst[m % 2], 16 * (n_tiles // 2))
                if m >= 2:
                    act.wait_ge(s_yst[m % 2], 16 * (m // 2))
                act.copy(y[m % 2][:], ps_b[m % 2][:]).then_inc(s_ycopy, 1)

            for m in range(SH):
                if m:
                    zT_hi_of(m - 1)
                silu_of(m)
                if m >= 2:
                    share_out(m - 2)
                if m in ACT_AV:
                    for t in ACT_AV[m]:
                        act.wait_ge(s_eq, t + 1)
                        act.activation(AV[:, t, 0], AV[:, t, 1], ACT.Copy, scale=const["token1"]).then_inc(s_av, 1)
                if m == SPLIT_AT:
                    act.wait_ge(s_rawgu[0], 16)
                    for p in PIECES:
                        act.copy(gu_hi[:, 0, p], raw_gu[0][:, p]).then_inc(s_guhi, 1)
                    act.wait_ge(s_rawd[0], 16)
                    act.copy(d_hi[:, 0], raw_d[0][:]).then_inc(s_dhi, 1)

            def row_hi(s):
                act.wait_ge(s_xgT, s + 1)
                act.wait_ge(s_up, SH + s - 1)
                act.copy(xT_hi[s % 2][:], ps_t[s % 2][:]).then_inc(s_xghi, 1)

            def weighted(s):
                act.wait_ge(s_down, SH + s + 1)
                act.wait_ge(s_cwsel, s + 1)
                if s < 2:
                    act.wait_ge(s_yst[s % 2], 16 * (SH // 2))
                else:
                    act.wait_ge(s_scat, 16 * (s - 1))
                act.activation(y[s % 2][:], ps_b[s % 2][:], ACT.Copy, scale=cw_col[:, s:s + 1]).then_inc(s_yex, 1)

            share_out(SH - 2)
            row_hi(0)
            after = Next(act)

            def d_high(s):
                def split(i):
                    act.wait_ge(s_rawd[i], after.loads(s - 1))
                    act.wait_ge(s_down, SH + s - 1)
                    act.copy(d_hi[:, i], raw_d[i][:]).then_inc(s_dhi, 1)
                after.split(s - 1, s_dhi, s, 1, split)

            def high(s):
                def others():
                    zT_hi_of(SH + s - 1)
                    if s >= 2:
                        weighted(s - 2)

                def split(i):
                    act.wait_ge(s_rawgu[i], after.loads(s))
                    act.wait_ge(s_up, SH + s)
                    act.copy(gu_hi[:, i, PIECES[0]], raw_gu[i][:, PIECES[0]]).then_inc(s_guhi, 1)
                    others()
                    act.copy(gu_hi[:, i, PIECES[1]], raw_gu[i][:, PIECES[1]]).then_inc(s_guhi, 1)
                    row_hi(s + 1)

                def keep():
                    act.wait_ge(s_guhi, 2 * (s + 1))
                    act.sem_inc(s_guhi, 2)
                    others()
                    row_hi(s + 1)
                after.branch(s, split, keep)

            def inner(s):
                if s:
                    d_high(s)
                high(s)
                after.look(s + 1)
                silu_of(SH + s)
                if s == 0:
                    share_out(SH - 1)

            def last(s):
                d_high(s)
                zT_hi_of(SH + s - 1)
                weighted(s - 2)
                silu_of(SH + s)
                weighted(s - 1)
                zT_hi_of(SH + s)
                weighted(s)

            after.look(0)
            slots(act, inner, last)

        @block.vector
        def _(dve):
            step = [0]

            def link(ins):
                step[0] += 1
                ins.then_inc(s_dve, 1)

            def linked():
                dve.wait_ge(s_dve, step[0])

            def chain(ins):
                link(ins)
                linked()

            def x_lo(t):
                if t >= n_tiles:
                    return
                dve.wait_ge(s_xhi, t + 1)
                if t >= 2:
                    dve.wait_ge(s_cond, t - 1)
                dve.tensor_tensor(xT_lo[t % 2][:], raw_xT[t % 2][:], xT_hi[t % 2][:], ALU.subtract).then_inc(s_xlo, 1)

            split = [0]

            def low_of(dst, src, high):
                split[0] += 1
                dve.wait_ge(s_whi, split[0])
                dve.tensor_tensor(dst, src, high, ALU.subtract).then_inc(s_wlo, 1)

            def route(j):
                tiles = range(PAIR * j, PAIR * (j + 1))
                at = slice(tiles.start, tiles.stop)
                dve.wait_ge(s_sig, j + 1)
                chain(dve.tensor_tensor(scores[:, at], scores[:, at], b_gate[:].unsqueeze(1).broadcast_to([P, PAIR, E]), ALU.add))
                for t in tiles:
                    link(dve.max(top8[:, t, :], scores[:, t, :]))
                linked()
                for t in tiles:
                    link(dve.max_index(idx8[:, t, :], top8[:, t, :], scores[:, t, :]))
                link(dve.tensor_reduce(wsum[:, at], top8[:, at, 0:TOPK], AX_X, ALU.add))
                linked()
                link(dve.tensor_copy(idxf[:], idx8[:, at]))
                chain(dve.tensor_scalar(winv[:, at], wsum[:, at], 1e-20, None, ALU.add))
                for n in range(PAIR):
                    link(dve.tensor_tensor(hot[:, n], idxf[:, n, 0:TOPK].unsqueeze(1).broadcast_to([P, E, TOPK]),
                                           const["expert"].unsqueeze(2).broadcast_to([P, E, TOPK]), ALU.is_equal))
                link(dve.reciprocal(wsum[:, at], winv[:, at]))
                linked()
                with nc.allow_low_precision(reason="0 and 1"):
                    dve.tensor_reduce(sel[:, at], hot[:], AX_X, ALU.add).then_inc(s_sel, 1)
                dve.wait_ge(s_sel, j + 1)
                for t in tiles:
                    dve.scalar_tensor_tensor(cw[:, t], sel[:, t].bitcast(F32), wsum[:, t:t + 1], scores[:, t],
                                             ALU.mult, ALU.mult).then_inc(s_cw, 1)

            def round_constants():
                dve.wait_ge(s_small, 16 * N_SMALL)
                link(dve.tensor_copy(before_r[:], const["before"]))
                link(dve.tensor_copy(ones_r[:], const["ones"]))
                link(dve.tensor_copy(column_b[:], const["column"].unsqueeze(2).broadcast_to([P, P, n_tiles])))
                link(dve.tensor_scalar(slot_b[:], const["slot"].unsqueeze(2).broadcast_to([P, NS, E]), float(MARK), None, ALU.add))

            x_lo(0)
            for p in PIECES:
                low_of(gu_lo[:, 0, p], raw_gu[0][:, p], gu_hi[:, 0, p])
            x_lo(1)
            dve.wait_ge(s_bias, 32)
            for t in range(n_tiles + 1):
                if t < n_tiles:
                    dve.wait_ge(s_cond, t + 1)
                    if t >= 2:
                        dve.wait_ge(s_hT, t - 1)
                        dve.wait_ge(s_hst[t % 2], 16 * (t // 2))
                    dve.scalar_tensor_tensor(h_nat[t % 2][:], ps_b[t % 2][:], c_col[:, t:t + 1], b_cond[:],
                                             ALU.mult, ALU.add).then_inc(s_h, 1)
                    dve.wait_ge(s_h, 2 * t + 1)
                    dve.tensor_tensor(h_nat[t % 2][:], h_nat[t % 2][:], ps_a[t % 2][:], ALU.add).then_inc(s_h, 1)
                x_lo(t + 2)
                if t == 0:
                    dve.wait_ge(s_gwhi, 1)
                    dve.tensor_tensor(gate_lo[:], raw_gate[:], gate_hi[:], ALU.subtract).then_inc(s_gwlo, 1)
                if t:
                    dve.wait_ge(s_hThi, t)
                    dve.tensor_tensor(hT_lo[:, t - 1], ps_t[(t - 1) % 2][:], hT_hi[:, t - 1], ALU.subtract).then_inc(s_hTlo, 1)
                if t == 1:
                    round_constants()
                for n in SPLIT_SHARED.get(t, ()):
                    low, high, raw = shared_piece(n)
                    low_of(low, raw, high)
                if t >= 2 * PAIR and t % PAIR == 0:
                    route(t // PAIR - 2)
            route(n_tiles // PAIR - 1)
            with nc.allow_low_precision(reason="counts up to the number of tiles"):
                dve.tensor_reduce(sel_all[:], sel[:].bitcast(F32).rearrange("p t e -> p e t"), AX_X, ALU.add).then_inc(s_sel, 1)
            dve.wait_ge(s_sign, n_tiles)

            def zmul(m):
                dve.wait_ge(s_silu, m + 1)
                dve.tensor_tensor(silu[m % 2][:], silu[m % 2][:], ps_a[m % 2][:, I:2 * I], ALU.mult).then_inc(s_zmul, 1)

            def zT_lo_of(m):
                dve.wait_ge(s_zhi, m + 1)
                if m >= 2:
                    dve.wait_ge(s_down, m - 1)
                dve.tensor_tensor(zT_lo[m % 2][:], ps_z[:, 0:I], zT_hi[m % 2][:], ALU.subtract).then_inc(s_zlo, 1)

            def counts():
                dve.wait_ge(s_pos, 1)
                pos, many = ps_g[:, 0:n_tiles * E], ps_g[:, n_tiles * E:n_tiles * E + E]
                link(dve.tensor_copy(pos_i[:], pos))
                chain(dve.tensor_scalar(nt_i[:], many, float(P - 1), None, ALU.add))
                link(dve.tensor_scalar(sl_i[:], pos_i[:], LOG_P, None, ALU.arith_shift_right))
                chain(dve.tensor_scalar(nt_i[:], nt_i[:], LOG_P, None, ALU.arith_shift_right))
                link(dve.tensor_scalar(pos_i[:], pos_i[:], P - 1, None, ALU.bitwise_and))
                chain(dve.tensor_copy(nt_f[:], nt_i[:]))
                link(dve.tensor_copy(sl_f[:], sl_i[:]))
                link(dve.tensor_copy(col_b[:].rearrange("p e t -> p t e"), pos_i[:].rearrange("p (t e) -> p t e", e=E)))
                chain(dve.tensor_tensor(tri, nt_f[:].unsqueeze(1).broadcast_to(by_e), upto, ALU.mult))
                link(dve.tensor_scalar(active[:], nt_f[:], 1.0, None, ALU.min))
                chain(dve.tensor_reduce(end_f[:], tri, AX_X, ALU.add))
                chain(dve.tensor_tensor(base_f[:], end_f[:], nt_f[:], ALU.subtract))
                chain(dve.tensor_tensor(sl_f[:], sl_f[:], base_f[:].unsqueeze(1).broadcast_to([P, n_tiles, E]), ALU.add))
                chain(dve.scalar_tensor_tensor(sl_b[:], sel[:].bitcast(F32), float(MARK), sl_f[:], ALU.mult, ALU.add))

            by_e, by_s, by_r = [P, E, E], [P, NS, E], [P, E + 2, E]
            upto = const["upto"].rearrange("p (a b) -> p a b", a=E)
            below = const["below"].rearrange("p (a b) -> p a b", a=E)

            def rank_runs():
                link(dve.tensor_scalar(ends[:], end_f[:], float(MARK), None, ALU.add))
                link(dve.tensor_scalar(bases[:], base_f[:], float(MARK), None, ALU.add))
                link(dve.tensor_copy(active_b[:], active[:]))
                chain(dve.tensor_tensor(tri, active[:].unsqueeze(1).broadcast_to(by_e), below, ALU.mult))
                for at_slot, bound in ((ended, ends), (begun, bases)):
                    dve.tensor_tensor(at_slot, slot_b[:], bound[:].unsqueeze(1).broadcast_to(by_s), ALU.is_ge)\
                        .then_inc(s_ranked, 1)
                dve.wait_ge(s_ranked, 1)
                link(dve.tensor_reduce(rank[:], tri, AX_X, ALU.add))
                link(dve.tensor_tensor(ended_a, ended, active_b[:].unsqueeze(1).broadcast_to(by_s), ALU.mult))
                link(dve.tensor_tensor(active_e[:], active[:], const["expert"], ALU.mult))
                linked()

            def name_runs():
                link(dve.tensor_tensor(active_e[:], active_e[:], active[:], ALU.add))
                link(dve.tensor_reduce(run_f[:], ended_a, AX_X, ALU.add))
                link(dve.tensor_tensor(at_run, rank[:].unsqueeze(1).broadcast_to(by_r),
                                       const["run"].unsqueeze(2).broadcast_to(by_r), ALU.is_equal))
                link(dve.scalar_tensor_tensor(last_run[:], active[:, E - 1:E], -1.0, rank[:, E - 1:E], ALU.add, ALU.add))
                linked()
                link(dve.tensor_tensor(at_run, at_run, active_e[:].unsqueeze(1).broadcast_to(by_r), ALU.mult))
                link(dve.memset(first[:, 0:1], 1.0))
                link(dve.tensor_tensor(first[:, 1:NS], run_f[:, 1:NS], run_f[:, 0:NS - 1], ALU.not_equal))
                link(dve.tensor_copy(run_i[:], run_f[0:1, :]))
                linked()
                link(dve.tensor_reduce(runs_f[:], at_run, AX_X, ALU.add))
                link(dve.tensor_scalar(run_odd[:], run_i[:], 1, None, ALU.bitwise_and))
                link(dve.tensor_copy(first_i[:], first[0:1, :]))
                link(dve.tensor_scalar(flags[:, 0, :], run_f[:], last_run[:, 0:1], None, ALU.is_lt))
                linked()

            def pack_words():
                link(dve.tensor_copy(runs_i[:], runs_f[0:1, :]))
                link(dve.tensor_tensor(flags[:, 0, :], flags[:, 0, :], first[:], ALU.mult))
                link(dve.tensor_copy(flags[0:1, 1, :], run_odd[:]))
                linked()
                chain(dve.tensor_tensor(flags[0:1], flags[0:1], const["power"][0:1].unsqueeze(1).broadcast_to([1, 2, NS]), ALU.mult))
                link(dve.tensor_copy(words_f[0:1, 0:1], end_f[0:1, E - 1:E]))
                chain(dve.tensor_reduce(words_f[0:1, 1:5], flags[0:1].rearrange("p k (w b) -> p (k w) b", w=2), AX_X, ALU.add))
                dve.tensor_copy(words[0:1, 0:5], words_f[0:1, 0:5]).then_inc(s_words, 1)

            def chosen():
                for t in range(n_tiles):
                    dve.tensor_tensor(AV[:, t, 1], sl_b[:, t].unsqueeze(1).broadcast_to(by_s), slot_b[:], ALU.is_equal)\
                        .then_inc(s_eq, 1)

            def tile_numbers(early):
                by_act = [t for m in ACT_AV for t in ACT_AV[m]]
                own = [t for t in range(n_tiles) if t not in by_act and t not in POOL_AV]
                if early:
                    dve.wait_ge(s_eq, n_tiles)
                    for t in own:
                        link(dve.tensor_scalar(AV[:, t, 0], AV[:, t, 1], const["token1"], None, ALU.mult))
                    linked()
                for t in (own if early else by_act + POOL_AV):
                    if t in by_act:
                        dve.wait_ge(s_av, by_act.index(t) + 1)
                    if t in POOL_AV:
                        dve.wait_ge(s_avp, POOL_AV.index(t) + 1)
                    dve.tensor_scalar(AV[:, t, 1], AV[:, t, 1], float(t), None, ALU.mult).then_inc(s_eq, 1)

            def columns(*experts):
                for e in experts:
                    if e >= 2:
                        dve.wait_ge(s_list, e - 1)
                    dve.tensor_tensor(B[e % 2], column_b[:], col_b[:, e, :].unsqueeze(1).broadcast_to([P, P, n_tiles]),
                                      ALU.is_equal).then_inc(s_B, 1)

            def indices():
                dve.wait_ge(s_list, E)
                chain(dve.tensor_copy(pad[:], ps_g[:, 0:NS]))
                chain(dve.scalar_tensor_tensor(found[:], ps_g[:, NS:2 * NS], float(P), pad[:], ALU.mult, ALU.add))
                link(dve.tensor_scalar(pad[:], found[:], 0.0, const["trash"], ALU.is_equal, ALU.mult))
                chain(dve.tensor_scalar(found[:], found[:], -1.0, None, ALU.add))
                dve.tensor_scalar(take_i[:], found[:], 0.0, None, ALU.max).then_inc(s_idx, 1)
                dve.tensor_tensor(give_i[:], found[:], pad[:], ALU.add).then_inc(s_idx, 1)

            for m in range(SH):
                if m:
                    zT_lo_of(m - 1)
                zmul(m)
                if m == 0:
                    counts()
                if m == 1:
                    chosen()
                if m == 2:
                    columns(0, 1)
                    tile_numbers(True)
                if m == 3:
                    tile_numbers(False)
                    rank_runs()
                    columns(2, 3)
                if m == 4:
                    name_runs()
                    columns(4, 5)
                if m == 5:
                    pack_words()
                    columns(*range(6, 12))
                if m == 6:
                    columns(*range(12, E))
                    indices()
                if m == SPLIT_AT:
                    first_run_low(dve, 1, s_gulo, 2)

            def row_lo(s):
                dve.wait_ge(s_gath[s % AHEAD], 16 * (s // AHEAD + 1))
                if s:
                    dve.wait_ge(s_cwsel, s)
                dve.tensor_tensor_reduce(cw_row[:], xg[s % AHEAD][:, H:ROW], hot_e[:, s, :], 1.0, 0.0, ALU.mult, ALU.add,
                                         cw_col[:, s:s + 1]).then_inc(s_cwsel, 1)
                dve.wait_ge(s_xghi, s + 1)
                dve.wait_ge(s_up, SH + s - 1)
                dve.tensor_tensor(xT_lo[s % 2][:], ps_t[s % 2][:], xT_hi[s % 2][:], ALU.subtract).then_inc(s_xglo, 1)

            dve.wait_ge(s_hot, 1)
            row_lo(0)
            after = Next(dve)

            def low(s):
                def piece(i, n):
                    dve.wait_ge(s_guhi, 2 * (s + 1) + n + 1)
                    p = PIECES[n]
                    dve.tensor_tensor(gu_lo[:, i, p], raw_gu[i][:, p], gu_hi[:, i, p], ALU.subtract).then_inc(s_gulo, 1)

                def split(i):
                    dve.wait_ge(s_up, SH + s)
                    piece(i, 0)
                    zT_lo_of(SH + s - 1)
                    piece(i, 1)
                    row_lo(s + 1)

                def keep():
                    dve.wait_ge(s_gulo, 2 * (s + 1))
                    dve.sem_inc(s_gulo, 2)
                    zT_lo_of(SH + s - 1)
                    row_lo(s + 1)
                after.branch(s, split, keep)

            def inner(s):
                low(s)
                after.look(s + 1)
                zmul(SH + s)

            def last(s):
                zT_lo_of(SH + s - 1)
                zmul(SH + s)
                zT_lo_of(SH + s)

            after.look(0)
            slots(dve, inner, last)

        @block.tensor
        def _(pe):
            def product(dst, pairs, which=None):
                n = len(pairs)
                for i in which or range(n):
                    lhs, rhs = pairs[i]
                    last = pe.matmul(dst, lhs, rhs, start=(i == 0), stop=(i == n - 1))
                return last

            def three(lhi, llo, rhi, rlo, chunks):
                return [(lhs[:, k], rhs(k)) for lhs, rhs in ((lhi, rhi), (lhi, rlo), (llo, rhi)) for k in range(chunks)]

            def fixed(w, *at):
                return lambda k: w[(slice(None),) + at + (k,)]

            def cond(t):
                pe.wait_ge(s_xhi, t + 1)
                if t >= 2:
                    pe.wait_ge(s_h, 2 * (t - 1))
                i = t % 2
                pairs = three(xT_hi[i], xT_lo[i], fixed(gu_hi, 0), fixed(gu_lo, 0), KH)
                half = KH // 2
                for n in range(2):
                    pe.wait_ge(s_whi, n + 1)
                    product(ps_a[i][:], pairs, range(n * half, (n + 1) * half))
                for n in range(2):
                    pe.wait_ge(s_wlo, n + 1)
                    product(ps_a[i][:], pairs, range(KH + n * half, KH + (n + 1) * half))
                pe.wait_ge(s_xlo, t + 1)
                product(ps_a[i][:], pairs, range(2 * KH, 3 * KH))
                pe.wait_ge(s_sign, t + 1)
                product(ps_b[i][:], [(h[i][:, k], sign[i][:, k]) for h in (xT_hi, xT_lo) for k in range(KH)]).then_inc(s_cond, 1)

            def turn(t):
                pe.wait_ge(s_h, 2 * (t + 1))
                pe.wait_ge(s_small, 16 * N_SMALL)
                if t >= 2:
                    pe.wait_ge(s_hTlo, t - 1)
                for k in range(KH):
                    last = pe.transpose(ps_t[t % 2][:, k * P:(k + 1) * P], h_nat[t % 2][:, k * P:(k + 1) * P], const["ident"])
                last.then_inc(s_hT, 1)

            def gate(t):
                pe.wait_ge(s_hThi, t + 1)
                pe.wait_ge(s_hTlo, t + 1)
                pe.wait_ge(s_gwlo, 1)
                j = t // PAIR
                if j >= 2:
                    pe.wait_ge(s_sig, j - 1)
                product(ps_gate[j % 2][:, t * E:(t + 1) * E], three(hT_hi[:, t], hT_lo[:, t], fixed(gate_hi), fixed(gate_lo), KH))\
                    .then_inc(s_gate, 1)

            UP = 3 * KH
            THIRDS = [range(0, UP // 3), range(UP // 3, 2 * UP // 3), range(2 * UP // 3, UP)]

            def up_pairs(m, gh, gl):
                if m < SH:
                    return three(hT_hi[:, m], hT_lo[:, m], gh, gl, KH)
                i = m % 2
                return three(xT_hi[i], xT_lo[i], gh, gl, KH)

            def up(m, pairs, part):
                if part == 0 and m >= 2:
                    pe.wait_ge(s_zmul, m - 1)
                last = product(ps_a[m % 2][:], pairs, THIRDS[part])
                if part == 2:
                    last.then_inc(s_up, 1)

            sh_gu = (fixed(gu_hi, 1), fixed(gu_lo, 1))
            sh_d = (fixed(d_hi, 1), fixed(d_lo, 1))
            for t in range(n_tiles + 2):
                if t < n_tiles:
                    cond(t)
                if t == n_tiles:
                    pe.wait_ge(s_h, 2 * (n_tiles - 1))
                    pe.wait_ge(s_whi, N_SPLIT)
                    pe.wait_ge(s_wlo, N_SPLIT)
                    up(0, up_pairs(0, *sh_gu), 0)
                if 1 <= t <= n_tiles:
                    turn(t - 1)
                if t >= 2:
                    gate(t - 2)

            def turn_z(m):
                pe.wait_ge(s_zmul, m + 1)
                if m == 0:
                    pe.wait_ge(s_sig, n_tiles // PAIR)
                if m:
                    pe.wait_ge(s_zlo, m)
                for k in range(KI):
                    last = pe.transpose(ps_z[:, k * P:(k + 1) * P], silu[m % 2][:, k * P:(k + 1) * P], const["ident"])
                last.then_inc(s_zT, 1)

            def down(m, dh, dl):
                s = m - SH
                pe.wait_ge(s_zhi, m + 1)
                if s >= 0:
                    pe.wait_ge(s_dhi, s + 1)
                if 2 <= m < SH + 2:
                    pe.wait_ge(s_ycopy, m - 1)
                elif m >= SH + 2:
                    pe.wait_ge(s_yex, m - SH - 1)
                pairs = three(zT_hi[m % 2], zT_lo[m % 2], dh, dl, KI)
                product(ps_b[m % 2][:], pairs, range(0, KI))
                if s >= 0:
                    pe.wait_ge(s_dlo, s + 1)
                product(ps_b[m % 2][:], pairs, range(KI, 2 * KI))
                pe.wait_ge(s_zlo, m + 1)
                product(ps_b[m % 2][:], pairs, range(2 * KI, 3 * KI)).then_inc(s_down, 1)

            def positions():
                pe.wait_ge(s_sel, n_tiles // PAIR + 1)
                pe.wait_ge(s_sig, n_tiles // PAIR)
                flat = sel[:].rearrange("p t e -> p (t e)")
                for t in range(n_tiles - 1):
                    n = n_tiles - 1 - t
                    pe.matmul(ps_g[:, (t + 1) * E:n_tiles * E], ones_r[:], sel[:, t:t + 1, :].broadcast_to([P, n, E]),
                              start=(t == 0), stop=False, skip_group_check=True)
                pe.matmul(ps_g[:, 0:n_tiles * E], before_r[:], flat, start=False, stop=True, skip_group_check=True)
                pe.matmul(ps_g[:, n_tiles * E:n_tiles * E + E], ones_r[:], sel_all[:], start=True, stop=True,
                          skip_group_check=True).then_inc(s_pos, 1)

            def make_list(e):
                pe.wait_ge(s_B, e + 1)
                pe.wait_ge(s_eq, 2 * n_tiles)
                for t in range(n_tiles):
                    last = pe.matmul(ps_g[:, 0:2 * NS], B[e % 2][:, :, t], AV[:, t, :, :, e],
                                     start=(e == 0 and t == 0), stop=(e == E - 1 and t == n_tiles - 1))
                last.then_inc(s_list, 1)

            def turn_rows(s):
                pe.wait_ge(s_gath[s % AHEAD], 16 * (s // AHEAD + 1))
                if s >= 2:
                    pe.wait_ge(s_xglo, s - 1)
                for k in range(KH):
                    last = pe.transpose(ps_t[s % 2][:, k * P:(k + 1) * P], xg[s % AHEAD][:, k * P:(k + 1) * P], const["ident"])
                last.then_inc(s_xgT, 1)

            pe.wait_ge(s_h, 2 * n_tiles)
            pe.wait_ge(s_hTlo, n_tiles)
            for m in range(SH):
                pairs = up_pairs(m, *sh_gu)
                if m:
                    up(m, pairs, 0)
                if m == 1:
                    positions()
                if m:
                    turn_z(m - 1)
                up(m, pairs, 1)
                up(m, pairs, 2)
                if m:
                    down(m - 1, *sh_d)
                if m == max(lists_after):
                    count = slots_in_use(pe)
                    odd_words = flag_words(pe, 1)
                for e in lists_after.get(m, ()):
                    make_list(e)

            turn_rows(0)
            pe.wait_ge(s_firstlo, 1)

            def run_weights(s):
                odd = flag(odd_words, s)
                g = pe.snap(odd * (KH * 2 * I), min_val=0, max_val=KH * 2 * I)
                d = pe.snap(odd * (KI * H), min_val=0, max_val=KI * H)

                def moving(w, base, n):
                    flat = w[:].rearrange("p w k n -> p (w k n)")
                    return lambda k: flat[:, bass.ds(base + k * n, n)]

                return ((moving(gu_hi, g, 2 * I), moving(gu_lo, g, 2 * I)), (moving(d_hi, d, H), moving(d_lo, d, H)))

            d_of = {-1: sh_d}

            def begin(s):
                gu_w, d_of[s] = run_weights(s)
                m = SH + s
                pairs = up_pairs(m, *gu_w)
                pe.wait_ge(s_guhi, 2 * (s + 1))
                pe.wait_ge(s_xghi, s + 1)
                up(m, pairs, 0)
                turn_z(m - 1)
                pe.wait_ge(s_gulo, 2 * (s + 1))
                up(m, pairs, 1)

                def finish():
                    pe.wait_ge(s_xglo, s + 1)
                    up(m, pairs, 2)
                    down(m - 1, *d_of[s - 1])
                return finish

            def inner(s):
                finish = begin(s)
                turn_rows(s + 1)
                finish()

            def last(s):
                begin(s)()
                turn_z(SH + s)
                down(SH + s, *d_of[s])

            slots(pe, inner, last, count)


def kernel(x, condB_coeff, mask_Bx4096x4096_ik1, L0_cond_W, L0_cond_b, L0_ffn_gate_w, L0_ffn_bias,
           L0_ffn_Wg, L0_ffn_Wu, L0_ffn_Wd, L0_ffn_Sg, L0_ffn_Su, L0_ffn_Sd):
    import numpy as np
    import concourse.bacc as bacc
    from concourse.bass_utils import run_bass_kernel_spmd

    def rows(a):
        a = np.asarray(a)
        a = a.reshape(*a.shape[:-2], a.shape[-2] // P, P, a.shape[-1])
        return np.ascontiguousarray(np.swapaxes(a, -3, -2))

    def turned(a):
        return rows(np.swapaxes(np.asarray(a), -1, -2))

    def spread(a):
        return np.ascontiguousarray(np.broadcast_to(np.asarray(a), (P, a.shape[0])))

    def constants(E, n_tokens):
        i, n = np.arange(P), 2 * WORD_BITS
        e = np.arange(E)
        row = {
            "ident": i[:, None] == i, "before": i[:, None] < i, "ones": np.ones((P, P)), "column": i,
            "slot": np.arange(n), "power": 2.0 ** (np.arange(n) % WORD_BITS), "expert": e,
            "upto": (e[None] <= e[:, None]).ravel(), "below": (e[None] < e[:, None]).ravel(),
            "run": np.arange(E + 2), "token1": i[:, None] + 1, "trash": n_tokens + 1 + i[:, None],
        }
        return np.concatenate([np.broadcast_to(row[k], (P, w)).astype(np.float32)
                               for k, w in const_layout(E, n).items()], axis=1)

    arrays = {
        "xT": turned(x),
        "x": np.ascontiguousarray(x),
        "coeff": spread(condB_coeff),
        "mask": rows(mask_Bx4096x4096_ik1),
        "WT": turned(L0_cond_W),
        "bias_cond": spread(L0_cond_b),
        "gateT": turned(L0_ffn_gate_w),
        "bias_gate": spread(L0_ffn_bias),
        "WguT": turned(np.concatenate([np.asarray(L0_ffn_Wg), np.asarray(L0_ffn_Wu)], axis=1)),
        "WdT": turned(L0_ffn_Wd),
        "SguT": turned(np.concatenate([np.asarray(L0_ffn_Sg), np.asarray(L0_ffn_Su)], axis=0)),
        "SdT": turned(L0_ffn_Sd),
        "consts": constants(L0_ffn_gate_w.shape[0], x.shape[0] * x.shape[1]),
    }
    nc = bacc.Bacc("TRN2", target_bir_lowering=False, num_devices=1)
    args = [nc.dram_tensor(n, a.shape, mybir.dt.from_np(a.dtype), kind="ExternalInput").ap() for n, a in arrays.items()]
    n_tokens, H = x.shape[0] * x.shape[1], x.shape[2]
    out = nc.dram_tensor("out", (n_tokens + P, H), F32, kind="ExternalOutput").ap()
    adaln_ffn(nc, *args, out)
    r = run_bass_kernel_spmd(nc, [arrays], core_ids=[0])
    return r.results[0]["out"][:n_tokens].reshape(x.shape)
```
